# Optimizing a Trainium2 kernel written in Bass

```python
import numpy as np
import jax
import jax.numpy as jnp

def _softmax(x, axis=-1):
    return jax.nn.softmax(x, axis=axis)

def _gelu(x):
    return jax.nn.gelu(x, approximate=True)

def _silu(x):
    return jax.nn.silu(x)

def _sigmoid(x):
    return jax.nn.sigmoid(x)

def _layernorm(x, axis=-1, eps=1e-05):
    m = jnp.mean(x, axis=axis, keepdims=True)
    v = jnp.var(x, axis=axis, keepdims=True)
    return (x - m) / jnp.sqrt(v + eps)

def _scatter_add(tgt, idx, src, axis=0):
    return tgt.at[idx].add(src)

def _segment_sum(src, seg, n):
    return jax.ops.segment_sum(src, seg, n)
kernel_name = 'mk_adaln_attn_ffn_d1_seqx_r8_d73c9f'

def setup_inputs(seed: int=0):
    np.random.seed(seed)
    _w = jnp.asarray

    def _rec_inputs():
        import jax
        import jax.numpy as jnp
        _rk = jax.random.key(seed)
        x = -7.109e-05 + 0.9999 * jax.random.normal(jax.random.fold_in(_rk, 1), (32, 128, 128), jnp.float32)
        _lenS = 128 - jax.random.randint(jax.random.fold_in(_rk, 7), (32,), 0, max(1, 128 // 4) + 1, jnp.int32)
        _lenS2 = 128 - jax.random.randint(jax.random.fold_in(_rk, 8), (32,), 0, max(1, 128 // 4) + 1, jnp.int32)
        cond_1024 = 0.00782532 + 1.00527 * jax.random.normal(jax.random.fold_in(_rk, 11), (32, 128), jnp.float32)
        return (x, cond_1024)
    x, cond_1024 = _rec_inputs()

    def _L0_cond_setup():
        import jax, jax.numpy as jnp
        import numpy as np
        B, S, T = (8, 1024, 1)
        SRC_DIM = 128
        TGT_DIM = 128
        NUM_HEADS = 16
        key = jax.random.key(seed)
        ks = jax.random.split(key, 12)
        sc_in = 1.0 / np.sqrt(SRC_DIM)
        sc_tg = 1.0 / np.sqrt(TGT_DIM)
        return {'query': jax.random.normal(ks[0], (B, S, SRC_DIM), dtype=jnp.float32), 'target': jax.random.normal(ks[1], (B, T, TGT_DIM), dtype=jnp.float32), 'Wq': jax.random.normal(ks[2], (SRC_DIM, TGT_DIM), dtype=jnp.float32) * sc_in, 'bq': jax.random.normal(ks[3], (TGT_DIM,), dtype=jnp.float32) * 0.01, 'Wk': jax.random.normal(ks[4], (TGT_DIM, TGT_DIM), dtype=jnp.float32) * sc_tg, 'bk': jax.random.normal(ks[5], (TGT_DIM,), dtype=jnp.float32) * 0.01, 'Wv': jax.random.normal(ks[6], (TGT_DIM, TGT_DIM), dtype=jnp.float32) * sc_tg, 'bv': jax.random.normal(ks[7], (TGT_DIM,), dtype=jnp.float32) * 0.01, 'Wo': jax.random.normal(ks[8], (TGT_DIM, SRC_DIM), dtype=jnp.float32) * sc_tg, 'bo': jax.random.normal(ks[9], (SRC_DIM,), dtype=jnp.float32) * 0.01, 'num_heads': NUM_HEADS}
    _L0_cond_all = _L0_cond_setup()
    _L0_cond_in = {k: v for k, v in _L0_cond_all.items() if k in ('Wq', 'bq', 'Wk', 'bk', 'Wv', 'bv', 'Wo', 'bo')}
    del _L0_cond_all

    def _L0_attn_setup():
        import jax, jax.numpy as jnp
        import numpy as np
        DIM = 128
        HEADS = 16
        EPS = 1e-06
        key = jax.random.key(seed)
        ks = jax.random.split(key, 6)
        b, t = (2, 128)
        s = 1.0 / np.sqrt(DIM)
        return {'x': jax.random.normal(ks[0], (b, t, DIM), dtype=jnp.float32), 'Wq': jax.random.normal(ks[1], (DIM, DIM), dtype=jnp.float32) * s, 'Wk': jax.random.normal(ks[2], (DIM, DIM), dtype=jnp.float32) * s, 'Wv': jax.random.normal(ks[3], (DIM, DIM), dtype=jnp.float32) * s, 'Wo': jax.random.normal(ks[4], (DIM, DIM), dtype=jnp.float32) * s, 'bo': jax.random.normal(ks[5], (DIM,), dtype=jnp.float32) * 0.01}
    _L0_attn_all = _L0_attn_setup()
    _L0_attn_in = {k: v for k, v in _L0_attn_all.items() if k in ('Wq', 'Wk', 'Wv', 'Wo', 'bo')}
    del _L0_attn_all

    def _L0_cond2_setup():
        import jax, jax.numpy as jnp
        import numpy as np
        INPUT_DIM = 128
        LATENT_DIM = 128
        key = jax.random.key(seed)
        ks = jax.random.split(key, 8)
        B, T = (64, 64)
        concat_dim = INPUT_DIM + LATENT_DIM
        s = lambda fan_in: 1.0 / np.sqrt(fan_in)
        return {'x': jax.random.normal(ks[0], (B, T, INPUT_DIM), dtype=jnp.float32), 'h0': jax.random.normal(ks[1], (B, LATENT_DIM), dtype=jnp.float32), 'w_W': jax.random.uniform(ks[2], (concat_dim, 2 * LATENT_DIM), jnp.float32, -s(concat_dim), s(concat_dim)), 'w_b': jax.random.uniform(ks[3], (2 * LATENT_DIM,), jnp.float32, -s(concat_dim), s(concat_dim)), 'wx_W': jax.random.uniform(ks[4], (INPUT_DIM, LATENT_DIM), jnp.float32, -s(INPUT_DIM), s(INPUT_DIM)), 'wx_b': jax.random.uniform(ks[5], (LATENT_DIM,), jnp.float32, -s(INPUT_DIM), s(INPUT_DIM)), 'wh_W': jax.random.uniform(ks[6], (LATENT_DIM, LATENT_DIM), jnp.float32, -s(LATENT_DIM), s(LATENT_DIM)), 'wh_b': jax.random.uniform(ks[7], (LATENT_DIM,), jnp.float32, -s(LATENT_DIM), s(LATENT_DIM))}
    _L0_cond2_all = _L0_cond2_setup()
    _L0_cond2_in = {k: v for k, v in _L0_cond2_all.items() if k in ('w_W', 'w_b', 'wx_W', 'wx_b', 'wh_W', 'wh_b')}
    del _L0_cond2_all

    def _L0_ffn_setup():
        import jax, jax.numpy as jnp
        import numpy as np
        B, T, C = (4, 256, 128)
        NUM_EXPERTS = 8
        TOP_K = 2
        D_EXPERT = 4 * C * TOP_K // NUM_EXPERTS
        key = jax.random.key(seed)
        k0, k1, k2, k3 = jax.random.split(key, 4)
        x = jax.random.normal(k0, (B, T, C), dtype=jnp.float32)
        router_w = jax.random.normal(k1, (NUM_EXPERTS, C), dtype=jnp.float32) * 0.02
        w1_all = jax.random.normal(k2, (NUM_EXPERTS, C, D_EXPERT), dtype=jnp.float32) * 0.02
        w2_all = jax.random.normal(k3, (NUM_EXPERTS, D_EXPERT, C), dtype=jnp.float32) * 0.02
        return {'x': x, 'router_w': router_w, 'w1_all': w1_all, 'w2_all': w2_all}
    _L0_ffn_all = _L0_ffn_setup()
    _L0_ffn_in = {k: v for k, v in _L0_ffn_all.items() if k in ('router_w', 'w1_all', 'w2_all')}
    del _L0_ffn_all
    return {'x': x, 'cond_1024': cond_1024, 'L0_cond_Wq': _L0_cond_in['Wq'], 'L0_cond_bq': _L0_cond_in['bq'], 'L0_cond_Wk': _L0_cond_in['Wk'], 'L0_cond_bk': _L0_cond_in['bk'], 'L0_cond_Wv': _L0_cond_in['Wv'], 'L0_cond_bv': _L0_cond_in['bv'], 'L0_cond_Wo': _L0_cond_in['Wo'], 'L0_cond_bo': _L0_cond_in['bo'], 'L0_attn_Wq': _L0_attn_in['Wq'], 'L0_attn_Wk': _L0_attn_in['Wk'], 'L0_attn_Wv': _L0_attn_in['Wv'], 'L0_attn_Wo': _L0_attn_in['Wo'], 'L0_attn_bo': _L0_attn_in['bo'], 'L0_cond2_w_W': _L0_cond2_in['w_W'], 'L0_cond2_w_b': _L0_cond2_in['w_b'], 'L0_cond2_wx_W': _L0_cond2_in['wx_W'], 'L0_cond2_wx_b': _L0_cond2_in['wx_b'], 'L0_cond2_wh_W': _L0_cond2_in['wh_W'], 'L0_cond2_wh_b': _L0_cond2_in['wh_b'], 'L0_ffn_router_w': _L0_ffn_in['router_w'], 'L0_ffn_w1_all': _L0_ffn_in['w1_all'], 'L0_ffn_w2_all': _L0_ffn_in['w2_all']}

def reference(x, cond_1024, L0_cond_Wq, L0_cond_bq, L0_cond_Wk, L0_cond_bk, L0_cond_Wv, L0_cond_bv, L0_cond_Wo, L0_cond_bo, L0_attn_Wq, L0_attn_Wk, L0_attn_Wv, L0_attn_Wo, L0_attn_bo, L0_cond2_w_W, L0_cond2_w_b, L0_cond2_wx_W, L0_cond2_wx_b, L0_cond2_wh_W, L0_cond2_wh_b, L0_ffn_router_w, L0_ffn_w1_all, L0_ffn_w2_all):
    import jax
    import jax.numpy as jnp

    def _L0_cond_ref(query, target, Wq, bq, Wk, bk, Wv, bv, Wo, bo, num_heads):
        import jax, jax.numpy as jnp
        import numpy as np
        B, S, T = (8, 1024, 1)
        SRC_DIM = 128
        TGT_DIM = 128
        NUM_HEADS = 16
        b, s, _ = query.shape
        H = num_heads
        hd = Wq.shape[1] // H

        def shard(t):
            return t.reshape(b, -1, H, hd).transpose(0, 2, 1, 3)
        q = shard(query @ Wq + bq).reshape(b, H * s, hd)
        k = shard(target @ Wk + bk).reshape(b, H, hd).transpose(0, 2, 1)
        v = shard(target @ Wv + bv).reshape(b, H, hd)
        scores = jnp.einsum('bnd,bdh->bnh', q, k) / jnp.sqrt(jnp.asarray(hd, q.dtype))
        scores = jax.nn.softmax(scores, axis=-1)
        context = jnp.einsum('bnh,bhd->bnd', scores, v)
        context = context.transpose(0, 2, 1).reshape(b, s, H * hd)
        return context @ Wo + bo

    def _L0_attn_ref(x, Wq, Wk, Wv, Wo, bo):
        import jax, jax.numpy as jnp
        import numpy as np
        DIM = 128
        HEADS = 16
        EPS = 1e-06
        b, t, e = x.shape
        h = HEADS
        d = e // h
        q = x @ Wq
        k = x @ Wk
        v = x @ Wv
        mh = lambda z: z.reshape(b, t, h, d).transpose(0, 2, 1, 3)
        q, k, v = (mh(q), mh(k), mh(v))
        q = jax.nn.softmax(q, axis=-1)
        k = jax.nn.elu(k) + 1.0
        k_cumsum = jnp.cumsum(k, axis=1)[..., None]
        context = jnp.einsum('bhnd,bhne->bhnde', k, v)
        context = jnp.cumsum(context, axis=1)
        context = context / (k_cumsum + EPS)
        attn = jnp.einsum('bhnd,bhnde->bhne', q, context)
        attn = attn.transpose(0, 2, 1, 3).reshape(b, t, e)
        return attn @ Wo + bo

    def _L0_cond2_ref(x, h0, w_W, w_b, wx_W, wx_b, wh_W, wh_b):
        import jax, jax.numpy as jnp
        import numpy as np
        INPUT_DIM = 128
        LATENT_DIM = 128
        xT = jnp.swapaxes(x, 0, 1)

        def step(h, x_t):
            fused = jax.nn.sigmoid(jnp.concatenate([x_t, h], axis=-1) @ w_W + w_b)
            hidden_state, output_state = jnp.split(fused, 2, axis=-1)
            memory_state = x_t @ wx_W + wx_b + hidden_state * (h @ wh_W + wh_b)
            h_new = output_state * h + (1.0 - output_state) * jnp.tanh(memory_state)
            return (h_new, h_new)
        _, hs = jax.lax.scan(step, h0, xT)
        return jnp.swapaxes(hs, 0, 1)

    def _L0_ffn_ref(x, router_w, w1_all, w2_all):
        import jax, jax.numpy as jnp
        import numpy as np
        B, T, C = (4, 256, 128)
        NUM_EXPERTS = 8
        TOP_K = 2
        D_EXPERT = 4 * C * TOP_K // NUM_EXPERTS
        b, t, c = x.shape
        x_flat = x.reshape(-1, c)
        router_logits = x_flat @ router_w.T
        top_k_logits, top_k_idx = jax.lax.top_k(router_logits, TOP_K)
        router_probs = jax.nn.softmax(top_k_logits, axis=-1)
        hidden = jnp.einsum('nc,ecd->ned', x_flat, w1_all)
        hidden = jnp.square(jax.nn.relu(hidden))
        out_all = jnp.einsum('ned,edc->nec', hidden, w2_all)
        sel = jnp.take_along_axis(out_all, top_k_idx[:, :, None], axis=1)
        out = jnp.sum(sel * router_probs[:, :, None], axis=1)
        return out.reshape(b, t, c)
    x = x + _L0_attn_ref(_L0_cond_ref(x, cond_1024[:, None, :], L0_cond_Wq, L0_cond_bq, L0_cond_Wk, L0_cond_bk, L0_cond_Wv, L0_cond_bv, L0_cond_Wo, L0_cond_bo, 16), L0_attn_Wq, L0_attn_Wk, L0_attn_Wv, L0_attn_Wo, L0_attn_bo)
    x = x + _L0_ffn_ref(_L0_cond2_ref(x, cond_1024, L0_cond2_w_W, L0_cond2_w_b, L0_cond2_wx_W, L0_cond2_wx_b, L0_cond2_wh_W, L0_cond2_wh_b), L0_ffn_router_w, L0_ffn_w1_all, L0_ffn_w2_all)
    return x

_drawn_inputs = setup_inputs


def setup_inputs(seed=0):
    import zlib

    import numpy as np

    out = dict(_drawn_inputs(seed))
    spreads = {}
    factors = {'L0_cond_bq': 8.0,
     'L0_cond_bk': 8.0,
     'L0_cond_bv': 8.0,
     'L0_cond_bo': 8.0,
     'L0_attn_Wq': 7.764,
     'L0_attn_Wk': 3.754,
     'L0_attn_bo': 4.872,
     'L0_cond2_w_W': 8.0,
     'L0_cond2_w_b': 8.0,
     'L0_cond2_wx_W': 8.0,
     'L0_cond2_wx_b': 8.0,
     'L0_cond2_wh_W': 8.0,
     'L0_cond2_wh_b': 8.0,
     'L0_ffn_router_w': 8.0,
     'L0_ffn_w1_all': 8.0,
     'L0_ffn_w2_all': 8.0}
    for name, (base, spread) in spreads.items():
        noise = np.random.default_rng([zlib.crc32(name.encode()), seed]).standard_normal(out[name].shape)
        drawn = base * np.exp(spread * noise) if base else spread * noise
        out[name] = jnp.asarray(drawn.astype(out[name].dtype))
    for name, factor in factors.items():
        out[name] = (out[name] * factor).astype(out[name].dtype)
    return out
```

```python
from contextlib import ExitStack

import concourse.bass as bass
from concourse import mybir

F32 = mybir.dt.float32
BF16 = mybir.dt.bfloat16
ALU = mybir.AluOpType
ACT = mybir.ActivationFunctionType
AX = mybir.AxisListType

B, S, C = 32, 128, 128
H, D = 16, 8
NE, DE = 8, 128
P = 128
STEPS = 4
TILES = S // STEPS
TOK = STEPS * B
GROUP = 4
BODY = 2 * GROUP
LEAD, LAG = 4, 2
PEEL = 4
EPS = 1e-6
SCALE = float(D) ** -0.5


def ds(start, size):
    return bass.ds(start, size)


def at_least(engine, semaphore, count):
    if not isinstance(count, int) or count > 0:
        engine.wait_ge(semaphore, count)


def pipeline(engine, iteration):
    for t in range(-LEAD, PEEL):
        iteration(t, t % 2, lambda off, t=t: 0 <= t + off < TILES)
    with engine.Fori(0, (TILES - LEAD - PEEL) // 2) as it:
        for k in range(2):
            iteration(2 * it + PEEL + k, k, lambda off: True)
    for t in range(TILES - LEAD, TILES + LAG):
        iteration(t, t % 2, lambda off, t=t: 0 <= t + off < TILES)


def adaln_attention_recurrence_moe(nc, x, cond, cWq, cbq, cWk, cbk, cWv, cbv, cWo, cbo, aWq, aWk, aWv, aWo, abo,
                                   w_W, w_b, wx_W, wx_b, wh_W, wh_b, router_w, w1_all, w2_all, out):
    with ExitStack() as ctx:
        def sb(name, shape, dt=F32):
            return ctx.enter_context(nc.sbuf_tensor(name, shape, dt))

        def sem(name):
            return ctx.enter_context(nc.semaphore(name))

        bank = [ctx.enter_context(nc.psum_tensor(f"bank{i}", [P, 512], F32)) for i in range(8)]

        ZH, ZO, MEM, ROWS, QKV, ATT, HID, OUT = bank

        ident = sb("ident", [P, P])
        cwq, cwk, cwv, cwo = (sb(n, [P, P]) for n in ("cwq", "cwk", "cwv", "cwo"))
        aw_raw = sb("aw_raw", [P, 3, P])
        aw = sb("aw", [P, 3, P])
        awo = sb("awo", [P, P])
        gwx = sb("gwx", [P, 2 * P])
        gwh = sb("gwh", [P, 2 * P])
        wxw, whw_raw, whw = sb("wxw", [P, P]), sb("whw_raw", [P, P]), sb("whw", [P, P])
        w1 = sb("w1", [P, NE, DE])
        w2 = sb("w2", [P, NE, C])
        rout_raw, routT = sb("rout_raw", [NE, P]), sb("routT", [P, NE])
        brow = sb("brow", [5, P])
        bcol = sb("bcol", [P, 5])
        grow = sb("grow", [1, 4 * P])
        gres = sb("gres", [1, 2, 4 * P])
        gpart = sb("gpart", [1, 3, 4 * P], BF16)
        gbias = sb("gbias", [3, 4 * P], BF16)
        ones = sb("ones", [3, 2 * TOK], BF16)
        scan_mask = sb("scan_mask", [P, D * D + D, H])
        cond_raw, condT = sb("cond_raw", [B, P]), sb("condT", [P, B])
        kvT = sb("kvT", [P, 2, B])
        m_head = sb("m_head", [P, H])
        m_dim = sb("m_dim", [P, D])
        m_hl = sb("m_hl", [P, D])
        rep_d = sb("rep_d", [P, P])
        rep_h = sb("rep_h", [P, P])
        kmask = sb("kmask", [P, H, B])
        vmask = sb("vmask", [P, D, B])
        kr = sb("kr", [P, H, B])
        vr = sb("vr", [P, D + 1, B])
        vbd = sb("vbd", [P, B, D + 1, D])
        xin = sb("xin", [P, 2, GROUP, P])
        XT = sb("XT", [P, B, S])
        CTX = sb("CTX", [P, S, B])
        qT = sb("qT", [P, 2, GROUP * P])
        kbd = sb("kbd", [P, 4, H, H])
        smax = sb("smax", [P, 2, H])
        ssub = sb("ssub", [P, 2, H, H])
        sexp = sb("sexp", [P, 2, H * H])
        pT = sb("pT", [P, 2, H * H])
        srec = sb("srec", [P, 2, 2, D])
        yT = sb("yT", [P, TOK])
        qkv = sb("qkv", [P, 2, 3, D, H])
        qmax = sb("qmax", [P, H])
        ex_in = sb("ex_in", [P, 2, D, H])
        ex = sb("ex", [P, 2, 2, D, H])
        qsum = sb("qsum", [P, H])
        kv = sb("kv", [P, D * D + D, H])
        kvs = sb("kvs", [P, D * D + D, H])
        den = sb("den", [P, D, H])
        rden = sb("rden", [P, D, H])
        qn = sb("qn", [P, 2, D, H])
        qc = sb("qc", [P, D, D, H])
        att = sb("att", [P, H, D])
        attT = sb("attT", [P, TOK])
        x1T = sb("x1T", [P, 2, STEPS, B])
        th = sb("th", [P, B, 2])
        to = sb("to", [P, B])
        mem = sb("mem", [P, B, 2])
        tm = sb("tm", [P, B, 2])
        wo = sb("wo", [P, B, 2])
        h2 = sb("h2", [P, 2, STEPS, B, 2])
        x1 = sb("x1", [P, 2, C])
        lg = sb("lg", [P, NE])
        top = sb("top", [P, 8])
        dl, gex, eq, ceq, few, tie, sel, gw = (sb(n, [P, NE]) for n in
                                               ("dl", "gex", "eq", "ceq", "few", "tie", "sel", "gw"))
        unique, gsum, grec = (sb(n, [P, 1]) for n in ("unique", "gsum", "grec"))
        gate = sb("gate", [P, 2, NE])
        hid = sb("hid", [P, 2, 512])
        hsq = sb("hsq", [P, 2, 512])
        acc = sb("acc", [P, 2, C])

        x_in, w_in, w_late, gb_in, out_done = sem("x_in0"), sem("w_in"), sem("w_late"), sem("gb_in"), sem("out_done")
        x_in = [x_in, sem("x_in1")]
        consts, const_step, gsplit = sem("consts"), sem("const_step"), sem("gsplit")
        ct_ps, ct_sb, kv_ps, kv_sb, kvm, kvr_ps, kr_sb, vr_sb, vbd_ok, late_sb, h_init, rt_ps = (
            sem(n) for n in ("ct_ps", "ct_sb", "kv_ps", "kv_sb", "kvm", "kvr_ps", "kr_sb", "vr_sb", "vbd_ok",
                             "late_sb", "h_init", "rt_ps"))
        xT_ps, xT_sb, q_ps, q_sb = sem("xT_ps"), sem("xT_sb"), sem("q_ps"), sem("q_sb")
        kbd_ok, s_ps, s_max, s_sub, s_exp = sem("kbd_ok"), sem("s_ps"), sem("s_max"), sem("s_sub"), sem("s_exp")
        pT_ps, pT_sb, c_ps, c_rec, c_sb = sem("pT_ps"), sem("pT_sb"), sem("c_ps"), sem("c_rec"), sem("c_sb")
        y_ps, y_sb, qkv_ps, qkv_sb = sem("y_ps"), sem("y_sb"), sem("qkv_ps"), sem("qkv_sb")
        q_max, ex_ready, ex_done, k_ready, q_sum, k_sum = (
            sem(n) for n in ("q_max", "ex_ready", "ex_done", "k_ready", "q_sum", "k_sum"))
        kv_done, kv_sum, d_den, d_rec, qn_done, qc_done, a_red = (
            sem("kv_done"), sem("kv_sum"), sem("d_den"), sem("d_rec"), sem("qn_done"), sem("qc_done"), sem("a_red"))
        aT_ps, aT_sb, p_ps, x1_done, xz_done, x1t_ps, x1t_sb = (
            sem(n) for n in ("aT_ps", "aT_sb", "p_ps", "x1_done", "xz_done", "x1t_ps", "x1t_sb"))
        zh_ps, g_ps, zo_ps, th_done, to_done, m_done, w_done, oh_done, tm_done, h_done = (
            sem(n) for n in ("zh_ps", "g_ps", "zo_ps", "th_done", "to_done", "m_done", "w_done", "oh_done",
                             "tm_done", "h_done"))
        l_ps, l_sb, l_copy, l_dl, g_exp, g_chain, gw_done, gs_done, gr_done, g_done = (
            sem(n) for n in (
                "l_ps", "l_sb", "l_copy", "l_dl", "g_exp", "g_chain", "gw_done", "gs_done", "gr_done", "g_done"))
        hid_ps, hid_sb, hsq_sb, o_ps, o_acc = sem("hid_ps"), sem("hid_sb"), sem("hsq_sb"), sem("o_ps"), sem("o_acc")

        XTt = XT[:, :, :].rearrange("p b t -> p t b")
        CTXf = CTX[:, :, :].rearrange("p t b -> p (t b)")
        x_d = x.rearrange("(g j) s c -> g s j c", j=GROUP)
        out_d = out.rearrange("b (n l) c -> n l b c", l=STEPS)

        WEIGHTS = [(cond_raw[:, :], cond), (cwk[:, :], cWk), (cwv[:, :], cWv), (cwq[:, :], cWq)] + [
            (brow[i:i + 1, :], b.rearrange("(a n) -> a n", a=1)) for i, b in enumerate((cbq, cbk, cbv, cbo, abo))]
        LATE = [
            (cwo[:, :], cWo), (aw_raw[:, 0, :], aWq), (aw_raw[:, 1, :], aWk), (aw_raw[:, 2, :], aWv), (awo[:, :], aWo),
            (gwx[:, :], w_W[0:C, :]), (gwh[:, :], w_W[C:2 * C, :]), (wxw[:, :], wx_W), (whw_raw[:, :], wh_W),
            (grow[:, 0:2 * P], w_b.rearrange("(a n) -> a n", a=1)),
            (grow[:, 2 * P:3 * P], wx_b.rearrange("(a n) -> a n", a=1)),
            (grow[:, 3 * P:4 * P], wh_b.rearrange("(a n) -> a n", a=1)),
            (rout_raw[:, :], router_w),
            (w1[:, :, :], w1_all.rearrange("e c d -> c e d")), (w2[:, :, :], w2_all.rearrange("e d c -> d e c"))]
        W_ALL, LATE_ALL = 16 * len(WEIGHTS), 16 * len(LATE)

        block = ctx.enter_context(nc.Block())

        @block.sync
        def _(sp):
            def load_x(g, half):
                sp.dma_start(xin[:, half, :, :], x_d[g]).then_inc(x_in[half], 16)

            for dst, src in WEIGHTS[:2]:
                sp.dma_start(dst, src).then_inc(w_in, 16)
            for half in range(2):
                load_x(half, half)
            for dst, src in WEIGHTS[2:]:
                sp.dma_start(dst, src).then_inc(w_in, 16)
            for dst, src in LATE:
                sp.dma_start(dst, src).then_inc(w_late, 16)
            with sp.Fori(1, B // BODY) as it:
                for half in range(2):
                    sp.wait_ge(xT_ps, 2 * it + half - 1)
                    load_x(2 * it + half, half)
            sp.wait_ge(gsplit, 6)
            for i in range(3):
                sp.dma_start(gbias[i:i + 1, :], gpart[:, i, :]).then_inc(gb_in, 16)

            def store(t, p):
                at_least(sp, out_done, 16 * t)
                sp.wait_ge(o_acc, NE * t + NE)
                sp.dma_start(out_d[t], acc[:, p, :]).then_inc(out_done, 16)

            for t in range(2):
                store(t, t)
            with sp.Fori(1, TILES // 2) as it:
                for p in range(2):
                    store(2 * it + p, p)
            sp.wait_ge(out_done, 16 * TILES)

        @block.gpsimd
        def _(pool):
            n = [0]

            def link(ins):
                ins.then_inc(const_step, 1)
                n[0] += 1
                pool.wait_ge(const_step, n[0])

            def band(t, lo, hi, pattern, mult):
                link(pool.affine_select(out=t, in_=t, compare_op=ALU.is_ge, fill=0.0, base=-lo,
                                        pattern=pattern, channel_multiplier=mult))
                link(pool.affine_select(out=t, in_=t, compare_op=ALU.is_ge, fill=0.0, base=hi,
                                        pattern=[[-s, k] for s, k in pattern], channel_multiplier=-mult))

            link(pool.memset(ident[:, :], 1.0))
            band(ident[:, :], 0, 0, [[-1, P]], 1)
            link(pool.memset(m_head[:, :], 1.0))
            band(m_head[:, :], 0, D - 1, [[-D, H]], 1)
            link(pool.memset(m_hl[:, :], 1.0))
            band(m_hl[:, :], 0, H - 1, [[-H, D]], 1)
            link(pool.memset(m_dim[:, :], 0.0))
            for k in range(H):
                link(pool.affine_select(out=m_dim[:, :], in_=m_dim[:, :], compare_op=ALU.not_equal, fill=1.0,
                                        base=-D * k, pattern=[[-1, D]], channel_multiplier=1))
            link(pool.tensor_copy(rep_d[:, :].rearrange("p (h d) -> p h d", d=D),
                                  m_dim[:, :].unsqueeze(1).broadcast_to([P, H, D])))
            link(pool.tensor_copy(rep_h[:, :].rearrange("p (l h) -> p l h", h=H),
                                  m_head[:, :].unsqueeze(1).broadcast_to([P, D, H])))
            link(pool.memset(vr[:, D, :], 1.0))
            link(pool.memset(scan_mask[:, :, :], 1.0))
            link(pool.memset(scan_mask[:, :, 0:1], 0.0))
            link(pool.memset(ones[:, :], 1.0))
            link(pool.memset(th[:, :, :], 0.0))
            link(pool.memset(tm[:, :, :], 0.0))
            pool.memset(h2[:, :, :, :, :], 0.0).then_inc(consts, 1)

            def key_blocks(b, k):
                pool.tensor_tensor(kbd[:, k % 4, :, :], m_head[:, :].unsqueeze(2).broadcast_to([P, H, H]),
                                   kr[:, :, ds(b, 1)].rearrange("p h o -> p o h").broadcast_to([P, H, H]),
                                   ALU.mult).then_inc(kbd_ok, 1)

            pool.wait_ge(kr_sb, 1)
            for b in range(4):
                key_blocks(b, b)
            with pool.Fori(0, B // BODY - 1) as it:
                for k in range(BODY):
                    pool.wait_ge(s_ps, BODY * it + k + 1)
                    key_blocks(BODY * it + k + 4, k)
            for b in range(B - BODY + 4, B):
                pool.wait_ge(s_ps, b - 3)
                key_blocks(b, b)


            def split(ins):
                ins.then_inc(gsplit, 1)
                split.n += 1
                pool.wait_ge(gsplit, split.n)

            split.n = 0
            pool.wait_ge(w_late, LATE_ALL)
            split(pool.tensor_scalar(grow[:, 3 * P:], grow[:, 3 * P:], 0.5, None, ALU.mult))
            split(pool.tensor_copy(gpart[:, 0, :], grow[:, :]))
            split(pool.tensor_tensor(gres[:, 0, :], grow[:, :], gpart[:, 0, :], ALU.subtract))
            split(pool.tensor_copy(gpart[:, 1, :], gres[:, 0, :]))
            split(pool.tensor_tensor(gres[:, 1, :], gres[:, 0, :], gpart[:, 1, :], ALU.subtract))
            pool.tensor_copy(gpart[:, 2, :], gres[:, 1, :]).then_inc(gsplit, 1)

            def outer(t, p):
                pool.wait_ge(k_ready, t + 1)
                at_least(pool, kv_sum, t)
                pool.tensor_tensor(
                    kv[:, 0:D * D, :].rearrange("p (d e) h -> p d e h", d=D),
                    kv[:, D * D:, :].unsqueeze(2).broadcast_to([P, D, D, H]),
                    qkv[:, p, 2, :, :].unsqueeze(1).broadcast_to([P, D, D, H]), ALU.mult).then_inc(kv_done, 1)

            def weigh(t, p):
                pool.wait_ge(kv_sum, t + 1)
                pool.wait_ge(qn_done, t + 1)
                at_least(pool, a_red, t)
                pool.tensor_tensor(
                    qc[:, :, :, :], kvs[:, 0:D * D, :].rearrange("p (d e) h -> p d e h", d=D),
                    qn[:, p, :, :].unsqueeze(2).broadcast_to([P, D, D, H]), ALU.mult).then_inc(qc_done, 1)

            def iteration(t, par, has):
                if has(2):
                    weigh(t + 2, par)
                if has(3):
                    outer(t + 3, 1 - par)

            pipeline(pool, iteration)

        @block.tensor
        def _(pe):
            def mm(dst, w, rhs, start=True):
                return pe.matmul(dst, w, rhs, start=start, stop=True, skip_group_check=True)

            pe.wait_ge(consts, 1)
            pe.wait_ge(w_in, W_ALL)
            pe.transpose(bank[0][:, 0:B], cond_raw[:, :], ident[0:B, 0:B])
            pe.transpose(bank[0][:, B:B + 5], brow[:, :], ident[0:5, 0:5]).then_inc(ct_ps, 1)
            pe.wait_ge(ct_sb, 2)
            mm(bank[1][:, 0:B], cwk[:, :], condT[:, :])
            mm(bank[1][:, B:2 * B], cwv[:, :], condT[:, :]).then_inc(kv_ps, 1)
            pe.wait_ge(kvm, 2)
            mm(bank[2][:, :], rep_d[:, :], kmask[:, :, :].rearrange("p h b -> p (h b)"))
            mm(bank[3][:, 0:D * B], rep_h[:, :], vmask[:, :, :].rearrange("p d b -> p (d b)")).then_inc(kvr_ps, 1)

            def project(g, half):
                if half is not None:
                    pe.wait_ge(x_in[half], x_count(g, half))
                at_least(pe, xT_sb, g)
                for j in range(GROUP):
                    last = pe.transpose(bank[6][:, j * P:(j + 1) * P], xin[:, half, j, :], ident[:, :])
                last.then_inc(xT_ps, 1)
                pe.wait_ge(xT_sb, g + 1)
                at_least(pe, q_sb, g)
                mm(bank[7][:, :], cwq[:, :], XT[:, ds(GROUP * g, GROUP), :].rearrange("p b s -> p (b s)"))\
                    .then_inc(q_ps, 1)

            def x_count(g, half):
                return 16 * (g // 2 + 1) if isinstance(g, int) else 16 * g_pair[0] + 16

            g_pair = [None]

            def scores(b, k):
                if k % GROUP == 0:
                    pe.wait_ge(q_sb, b // GROUP + 1 if isinstance(b, int) else 2 * g_pair[0] + k // GROUP + 1)
                pe.wait_ge(kbd_ok, b + 1)
                at_least(pe, s_sub, b - 1)
                mm(bank[k % 2][:, 0:H * H], qT[:, k // GROUP, (k % GROUP) * P:(k % GROUP + 1) * P],
                   kbd[:, k % 4, :, :].rearrange("p h g -> p (h g)")).then_inc(s_ps, 1)

            def probs_T(b, k):
                pe.wait_ge(s_exp, b + 1)
                at_least(pe, pT_sb, b - 1)
                pe.transpose(bank[2 + k % 2][:, 0:P], sexp[:, k % 2, 0:P], ident[:, :])
                pe.transpose(bank[2 + k % 2][:, P:2 * P], sexp[:, k % 2, P:2 * P], ident[:, :]).then_inc(pT_ps, 1)

            def context(b, k):
                pe.wait_ge(pT_sb, b + 1)
                at_least(pe, c_sb, b - 1)
                for j in range(2):
                    last = mm(bank[4 + k % 2][:, j * 72:(j + 1) * 72], pT[:, k % 2, j * P:(j + 1) * P],
                              vbd[:, ds(b, 1), :, :].rearrange("p o d h -> p (o d h)"))
                last.then_inc(c_ps, 1)

            def first(it, start, end):
                g_pair[0] = it
                for k in range(BODY):
                    b = BODY * it + k
                    if k % GROUP == 1 and not (end and k > GROUP):
                        if k < GROUP:
                            project(2 * it + 1, 1)
                        else:
                            g_pair[0] = it + 1
                            project(2 * it + 2, 0)
                            g_pair[0] = it
                    if not (end and k == BODY - 1):
                        if k == BODY - 1:
                            g_pair[0] = it + 1
                        scores(b + 1, (k + 1) % BODY)
                        g_pair[0] = it
                    probs_T(b, k)
                    if not (start and k == 0):
                        context(b - 1, (k - 1) % BODY)

            project(0, 0)
            pe.wait_ge(kr_sb, 1)
            scores(0, 0)
            pe.wait_ge(vbd_ok, 1)
            first(0, True, False)
            with pe.Fori(1, B // BODY - 1) as it:
                first(it, False, False)
            first(B // BODY - 1, False, True)
            context(B - 1, BODY - 1)

            pe.wait_ge(w_late, LATE_ALL)
            pe.transpose(bank[6][:, 0:NE], rout_raw[:, :], ident[0:NE, 0:NE]).then_inc(rt_ps, 1)
            pe.wait_ge(late_sb, 3)
            pe.wait_ge(h_init, 2)
            pe.wait_ge(c_sb, B)
            pe.wait_ge(gb_in, 48)

            def h_of(p):
                return h2[:, p, :, :, 1].rearrange("p l b -> p (l b)")

            def y(t):
                at_least(pe, qkv_sb, t)
                mm(QKV[:, 0:P], cwo[:, :], CTXf[:, ds(TOK * t, TOK)]).then_inc(y_ps, 1)

            def qkv_of(t):
                pe.wait_ge(y_sb, t + 1)
                mm(QKV[:, P:], yT[:, :], aw[:, :, :].rearrange("p w n -> p (w n)")).then_inc(qkv_ps, 1)

            def att_T(t):
                pe.wait_ge(a_red, t + 1)
                at_least(pe, x1_done, t)
                pe.transpose(ATT[:, 0:P], att[:, :, :].rearrange("p h e -> p (h e)"), ident[:, :]).then_inc(aT_ps, 1)

            def project_out(t):
                pe.wait_ge(aT_sb, t + 1)
                mm(ATT[:, P:2 * P], awo[:, :], attT[:, :]).then_inc(p_ps, 1)

            def gates_x(t, p):
                xs = x1T[:, p, :, :].rearrange("p l b -> p (l b)")
                odd = MEM[:, 1:2 * TOK:2]
                pe.wait_ge(x1_done, t + 1)
                at_least(pe, th_done, STEPS * t)
                mm(ZH[:, 0:TOK], gbias[:, 0:P], ones[:, 0:TOK])
                mm(ZH[:, 0:TOK], gwx[:, 0:P], xs, start=False)
                at_least(pe, to_done, STEPS * t)
                mm(ZO[:, 0:TOK], gbias[:, P:2 * P], ones[:, 0:TOK])
                mm(ZO[:, 0:TOK], gwx[:, P:2 * P], xs, start=False)
                at_least(pe, m_done, STEPS * t)
                mm(MEM[:, 0:2 * TOK], gbias[:, 3 * P:], ones[:, :])
                mm(odd, gbias[:, 2 * P:3 * P], ones[:, 0:TOK], start=False)
                mm(odd, wxw[:, :], xs, start=False).then_inc(xz_done, 1)

            def x_rows(t, p):
                at_least(pe, l_sb, t)
                pe.transpose(ROWS[:, 0:P], x1T[:, p, :, :].rearrange("p l b -> p (l b)"), ident[:, :])\
                    .then_inc(x1t_ps, 1)

            def logits(t, p):
                pe.wait_ge(x1t_sb, t + 1)
                mm(ROWS[:, P:P + NE], h_of(p), routT[:, :]).then_inc(l_ps, 1)

            def hidden(t, p, half):
                pe.wait_ge(h_done, STEPS * t + STEPS)
                at_least(pe, hid_sb, 2 * t + half)
                for j in range(4):
                    last = mm(HID[:, j * P:(j + 1) * P], w1[:, 4 * half + j, :], h_of(p))
                last.then_inc(hid_ps, 1)

            def experts_out(t, half):
                pe.wait_ge(hsq_sb, 2 * t + half + 1)
                at_least(pe, o_acc, NE * t + 4 * half)
                for j in range(4):
                    last = mm(OUT[:, j * P:(j + 1) * P], hsq[:, half, j * P:(j + 1) * P], w2[:, 4 * half + j, :])
                last.then_inc(o_ps, 1)

            def step(t, p, s):
                at_least(pe, h_done, STEPS * t + s)
                h = h2[:, p, s - 1, :, 1] if s else h2[:, 1 - p, STEPS - 1, :, 1]
                mm(ZH[:, s * B:(s + 1) * B], gwh[:, 0:P], h, start=False).then_inc(zh_ps, 1)
                mm(MEM[:, 2 * s * B:2 * (s + 1) * B], whw[:, :], h.unsqueeze(2).broadcast_to([P, B, 2]),
                   start=False).then_inc(g_ps, 1)
                mm(ZO[:, s * B:(s + 1) * B], gwh[:, P:2 * P], h, start=False).then_inc(zo_ps, 1)

            def iteration(t, p, has):
                q = 1 - p
                if has(0):
                    step(t, p, 0)
                if has(1):
                    project_out(t + 1)
                if has(4):
                    y(t + 4)
                if has(-1):
                    hidden(t - 1, q, 0)
                if has(0):
                    step(t, p, 1)
                if has(4):
                    qkv_of(t + 4)
                if has(-1):
                    logits(t - 1, q)
                if has(-2):
                    experts_out(t - 2, 1)
                if has(0):
                    step(t, p, 2)
                if has(-1):
                    hidden(t - 1, q, 1)
                if has(0):
                    step(t, p, 3)
                if has(-1):
                    experts_out(t - 1, 0)
                if has(2):
                    att_T(t + 2)
                if has(0):
                    x_rows(t, p)
                if has(1):
                    gates_x(t + 1, q)

            pipeline(pe, iteration)

        @block.scalar
        def _(act):
            act.preload_act_table(ACT.Exp)
            act.wait_ge(ct_ps, 1)
            act.activation(condT[:, :], bank[0][:, 0:B], ACT.Copy).then_inc(ct_sb, 1)
            act.activation(bcol[:, :], bank[0][:, B:B + 5], ACT.Copy).then_inc(ct_sb, 1)
            act.wait_ge(kv_ps, 1)
            act.wait_ge(ct_sb, 2)
            for i in range(2):
                act.activation(kvT[:, i, :], bank[1][:, i * B:(i + 1) * B], ACT.Identity, bias=bcol[:, i + 1:i + 2])\
                    .then_inc(kv_sb, 1)

            def group_T(g):
                act.wait_ge(xT_ps, g + 1)
                act.activation(XT[:, ds(GROUP * g, GROUP), :].rearrange("p b s -> p (b s)"), bank[6][:, :], ACT.Copy)\
                    .then_inc(xT_sb, 1)

            def group_q(g, half):
                act.wait_ge(q_ps, g + 1)
                at_least(act, s_ps, GROUP * (g - 1))
                act.activation(qT[:, half, :], bank[7][:, :], ACT.Identity, bias=bcol[:, 0:1]).then_inc(q_sb, 1)

            def exps(b, k):
                act.wait_ge(s_sub, b + 1)
                at_least(act, pT_ps, b - 1)
                act.activation(sexp[:, k % 2, :], ssub[:, k % 2, :, :].rearrange("p h g -> p (h g)"), ACT.Exp,
                               scale=SCALE).then_inc(s_exp, 1)

            def probs_out(b, k):
                act.wait_ge(pT_ps, b + 1)
                at_least(act, c_ps, b - 1)
                act.activation(pT[:, k % 2, :], bank[2 + k % 2][:, 0:2 * P], ACT.Copy).then_inc(pT_sb, 1)

            def first(it, end):
                for k in range(BODY):
                    if k % GROUP == 1 and not (end and k > GROUP):
                        group_T(2 * it + k // GROUP + 1)
                        group_q(2 * it + k // GROUP + 1, 1 - k // GROUP)
                    exps(BODY * it + k, k)
                    probs_out(BODY * it + k, k)

            group_T(0)
            group_q(0, 0)
            act.wait_ge(kvr_ps, 1)
            act.activation(kr[:, :, :].rearrange("p h b -> p (h b)"), bank[2][:, :], ACT.Copy).then_inc(kr_sb, 1)
            act.activation(vr[:, 0:D, :].rearrange("p d b -> p (d b)"), bank[3][:, 0:D * B], ACT.Copy)\
                .then_inc(vr_sb, 1)
            first(0, False)
            with act.Fori(1, B // BODY - 1) as it:
                first(it, False)
            first(B // BODY - 1, True)

            act.wait_ge(w_late, LATE_ALL)
            for w in range(2):
                act.activation(aw[:, w, :].rearrange("p (d h) -> p d h", d=D),
                               aw_raw[:, w, :].rearrange("p (h d) -> p d h", d=D), ACT.Copy)
            act.activation(aw[:, 2, :].rearrange("p (d h) -> p d h", d=D),
                           aw_raw[:, 2, :].rearrange("p (h d) -> p d h", d=D), ACT.Copy).then_inc(late_sb, 2)
            act.wait_ge(rt_ps, 1)
            act.activation(routT[:, :], bank[6][:, 0:NE], ACT.Copy).then_inc(late_sb, 1)

            def y_out(t):
                act.wait_ge(y_ps, t + 1)
                at_least(act, qkv_ps, t)
                act.activation(yT[:, :], QKV[:, 0:P], ACT.Identity, bias=bcol[:, 3:4]).then_inc(y_sb, 1)

            def qkv_out(t, p):
                act.wait_ge(qkv_ps, t + 1)
                at_least(act, kv_done, t - 1)
                act.activation(qkv[:, p, :, :, :].rearrange("p w d h -> p (w d h)"), QKV[:, P:], ACT.Copy)\
                    .then_inc(qkv_sb, 1)

            def exp_qk(t, p):
                act.wait_ge(ex_ready, t + 1)
                at_least(act, qn_done, t - 1)
                act.activation(ex[:, p, :, :, :].rearrange("p w d h -> p (w d h)"),
                               ex_in[:, :, :, :].rearrange("p w d h -> p (w d h)"), ACT.Exp).then_inc(ex_done, 1)

            def att_out(t):
                act.wait_ge(aT_ps, t + 1)
                at_least(act, p_ps, t)
                act.activation(attT[:, :], ATT[:, 0:P], ACT.Copy).then_inc(aT_sb, 1)

            def x_rows_out(t, p):
                act.wait_ge(x1t_ps, t + 1)
                at_least(act, o_acc, NE * (t - 2) + 1)
                act.activation(x1[:, p, :], ROWS[:, 0:P], ACT.Copy).then_inc(x1t_sb, 1)

            def relu(t, half):
                act.wait_ge(hid_ps, 2 * t + half + 1)
                act.activation(hid[:, half, :], HID[:, :], ACT.Relu).then_inc(hid_sb, 1)

            def square(t, half):
                act.wait_ge(hid_sb, 2 * t + half + 1)
                at_least(act, o_ps, 2 * t + half - 1)
                act.activation(hsq[:, half, :], hid[:, half, :], ACT.Square).then_inc(hsq_sb, 1)

            def gate_exp(t):
                act.wait_ge(l_dl, t + 1)
                at_least(act, g_done, t)
                act.activation(gex[:, :], dl[:, :], ACT.Exp).then_inc(g_exp, 1)

            def gates(t, p, s):
                n = STEPS * t + s
                act.wait_ge(zh_ps, n + 1)
                at_least(act, m_done, n)
                act.activation(th[:, :, 1], ZH[:, s * B:(s + 1) * B], ACT.Tanh, scale=0.5).then_inc(th_done, 1)
                act.wait_ge(zo_ps, n + 1)
                at_least(act, w_done, n)
                act.activation(to[:, :], ZO[:, s * B:(s + 1) * B], ACT.Tanh, scale=0.5)\
                    .then_inc(to_done, 1)
                act.wait_ge(m_done, n + 1)
                at_least(act, h_done, n)
                act.activation(tm[:, :, 1], mem[:, :, 1], ACT.Tanh).then_inc(tm_done, 1)

            def iteration(t, p, has):
                q = 1 - p
                if has(0):
                    gates(t, p, 0)
                if has(-2):
                    square(t - 2, 1)
                if has(4):
                    y_out(t + 4)
                if has(0):
                    gates(t, p, 1)
                if has(-1):
                    relu(t - 1, 0)
                if has(4):
                    qkv_out(t + 4, p)
                if has(0):
                    gates(t, p, 2)
                if has(-1):
                    square(t - 1, 0)
                if has(0):
                    gates(t, p, 3)
                if has(-1):
                    relu(t - 1, 1)
                    gate_exp(t - 1)
                if has(4):
                    exp_qk(t + 4, p)
                if has(2):
                    att_out(t + 2)
                if has(0):
                    x_rows_out(t, p)

            pipeline(act, iteration)

        @block.vector
        def _(dve):
            dve.wait_ge(consts, 1)
            dve.wait_ge(kv_sb, 2)
            dve.tensor_tensor(kmask[:, :, :], m_head[:, :].unsqueeze(2).broadcast_to([P, H, B]),
                              kvT[:, 0, :].unsqueeze(1).broadcast_to([P, H, B]), ALU.mult).then_inc(kvm, 1)
            dve.tensor_tensor(vmask[:, :, :], m_dim[:, :].unsqueeze(2).broadcast_to([P, D, B]),
                              kvT[:, 1, :].unsqueeze(1).broadcast_to([P, D, B]), ALU.mult).then_inc(kvm, 1)
            dve.wait_ge(vr_sb, 1)
            dve.tensor_tensor(vbd[:, :, :, :], vr[:, :, :].rearrange("p d b -> p b d").unsqueeze(3)
                              .broadcast_to([P, B, D + 1, D]),
                              m_hl[:, :].unsqueeze(1).unsqueeze(1).broadcast_to([P, B, D + 1, D]), ALU.mult)\
                .then_inc(vbd_ok, 1)

            def softmax_in(b, k):
                sc = bank[k % 2][:, 0:H * H].rearrange("p (h g) -> p h g", g=H)
                dve.wait_ge(s_ps, b + 1)
                dve.tensor_reduce(smax[:, k % 2, :], sc, AX.X, ALU.max).then_inc(s_max, 1)
                dve.wait_ge(s_max, b + 1)
                at_least(dve, s_exp, b - 1)
                dve.tensor_tensor(ssub[:, k % 2, :, :], sc, smax[:, k % 2, :].unsqueeze(2).broadcast_to([P, H, H]),
                                  ALU.subtract).then_inc(s_sub, 1)

            def normalise(b, k):
                cp = bank[4 + k % 2][:, 0:144].rearrange("p (j d l) -> p j d l", j=2, d=D + 1)
                dve.wait_ge(c_ps, b + 1)
                dve.reciprocal(srec[:, k % 2, :, :], cp[:, :, D, :]).then_inc(c_rec, 1)
                dve.wait_ge(c_rec, b + 1)
                for j in range(2):
                    dst = CTX[:, :, ds(b, 1)].rearrange("p (d j l) o -> p j d (l o)", d=D, j=2)[:, j]
                    last = dve.tensor_tensor(dst, cp[:, j, 0:D, :],
                                             srec[:, k % 2, j, :].unsqueeze(1).broadcast_to([P, D, D]), ALU.mult)
                last.then_inc(c_sb, 1)

            def first(it, start, end):
                for k in range(BODY):
                    if not (end and k == BODY - 1):
                        softmax_in(BODY * it + k + 1, k + 1)
                    if not (start and k == 0):
                        normalise(BODY * it + k - 1, (k - 1) % BODY)

            softmax_in(0, 0)
            first(0, True, False)
            with dve.Fori(1, B // BODY - 1) as it:
                first(it, False, False)
            first(B // BODY - 1, False, True)
            normalise(B - 1, BODY - 1)
            dve.wait_ge(w_late, LATE_ALL)
            dve.tensor_scalar(whw[:, :], whw_raw[:, :], 0.5, None, ALU.mult).then_inc(h_init, 1)
            dve.tensor_copy(h2[:, 1, STEPS - 1, :, 1], condT[:, :]).then_inc(h_init, 1)

            def flat(ap):
                return ap.rearrange("p a b -> p (a b)")

            def qk_ready(t, p):
                dve.wait_ge(qkv_sb, t + 1)
                dve.tensor_reduce(qmax[:, :], qkv[:, p, 0, :, :].rearrange("p d h -> p h d"), AX.X, ALU.max)\
                    .then_inc(q_max, 1)
                at_least(dve, ex_done, t)
                dve.tensor_scalar(ex_in[:, 1, :, :], qkv[:, p, 1, :, :], 0.0, None, ALU.min)
                dve.wait_ge(q_max, t + 1)
                dve.tensor_tensor(ex_in[:, 0, :, :], qkv[:, p, 0, :, :],
                                  qmax[:, :].unsqueeze(1).broadcast_to([P, D, H]), ALU.subtract).then_inc(ex_ready, 1)

            def keys(t, p):
                dve.wait_ge(ex_done, t + 1)
                at_least(dve, kv_done, t)
                dve.scalar_tensor_tensor(out=kv[:, D * D:, :], in0=qkv[:, p, 1, :, :], scalar=0.0,
                                         in1=ex[:, p, 1, :, :], op0=ALU.max, op1=ALU.add).then_inc(k_ready, 1)
                dve.tensor_reduce(qsum[:, :], ex[:, p, 0, :, :].rearrange("p d h -> p h d"), AX.X, ALU.add)\
                    .then_inc(q_sum, 1)
                dve.wait_ge(k_ready, t + 1)
                dve.tensor_tensor_scan(flat(kvs[:, D * D:, :]), flat(scan_mask[:, D * D:, :]), flat(kv[:, D * D:, :]),
                                       0.0, ALU.mult, ALU.add).then_inc(k_sum, 1)
                dve.wait_ge(q_sum, t + 1)
                dve.wait_ge(k_sum, t + 1)
                dve.scalar_tensor_tensor(out=den[:, :, :], in0=kvs[:, D * D:, :], scalar=EPS,
                                         in1=qsum[:, :].unsqueeze(1).broadcast_to([P, D, H]), op0=ALU.add,
                                         op1=ALU.mult).then_inc(d_den, 1)

            def queries(t, p):
                dve.wait_ge(d_den, t + 1)
                dve.reciprocal(rden[:, :, :], den[:, :, :]).then_inc(d_rec, 1)
                dve.wait_ge(d_rec, t + 1)
                at_least(dve, qc_done, t - 1)
                dve.tensor_tensor(qn[:, p, :, :], ex[:, p, 0, :, :], rden[:, :, :], ALU.mult).then_inc(qn_done, 1)

            def sum_heads(t):
                dve.wait_ge(kv_done, t + 1)
                at_least(dve, qc_done, t)
                dve.tensor_tensor_scan(flat(kvs[:, 0:D * D, :]), flat(scan_mask[:, 0:D * D, :]),
                                       flat(kv[:, 0:D * D, :]), 0.0, ALU.mult, ALU.add).then_inc(kv_sum, 1)

            def add_dims(t):
                dve.wait_ge(qc_done, t + 1)
                at_least(dve, aT_ps, t)
                dve.tensor_reduce(att[:, :, :].rearrange("p h e -> p e h"),
                                  qc[:, :, :, :].rearrange("p d e h -> p e h d"), AX.X, ALU.add).then_inc(a_red, 1)

            def residual(t, p):
                dve.wait_ge(p_ps, t + 1)
                at_least(dve, x1t_ps, t - 1)
                at_least(dve, xz_done, t - 1)
                dve.scalar_tensor_tensor(out=x1T[:, p, :, :],
                                         in0=ATT[:, P:2 * P].rearrange("p (l b) -> p l b", b=B),
                                         scalar=bcol[:, 4:5], in1=XTt[:, ds(STEPS * t, STEPS), :],
                                         op0=ALU.add, op1=ALU.add).then_inc(x1_done, 1)

            def route(t):
                dve.wait_ge(l_ps, t + 1)
                dve.tensor_copy(lg[:, :], ROWS[:, P:P + NE]).then_inc(l_copy, 1)
                dve.max(top[:, :], ROWS[:, P:P + NE]).then_inc(l_sb, 1)
                dve.wait_ge(l_copy, t + 1)
                dve.wait_ge(l_sb, t + 1)
                at_least(dve, g_exp, t)
                dve.tensor_scalar(dl[:, :], lg[:, :], top[:, 0:1], None, ALU.subtract).then_inc(l_dl, 1)

            def choose(t, p):
                base = 6 * t
                second = top[:, 1:2]
                dve.tensor_scalar(eq[:, :], lg[:, :], second, None, ALU.is_equal).then_inc(g_chain, 1)
                dve.tensor_scalar(unique[:, :], top[:, 0:1], second, -1.0, ALU.is_gt, ALU.mult).then_inc(g_chain, 1)
                dve.wait_ge(g_chain, base + 1)
                dve.tensor_tensor_scan(ceq[:, :], scan_mask[:, 0, 1:1 + NE], eq[:, :], 0.0, ALU.mult, ALU.add)\
                    .then_inc(g_chain, 1)
                dve.wait_ge(g_chain, base + 3)
                dve.tensor_scalar(few[:, :], ceq[:, :], unique[:, 0:1], 2.0, ALU.subtract, ALU.is_le)\
                    .then_inc(g_chain, 1)
                dve.wait_ge(g_chain, base + 4)
                dve.tensor_tensor(tie[:, :], few[:, :], eq[:, :], ALU.mult).then_inc(g_chain, 1)
                dve.wait_ge(g_chain, base + 5)
                dve.scalar_tensor_tensor(out=sel[:, :], in0=lg[:, :], scalar=second, in1=tie[:, :], op0=ALU.is_gt,
                                         op1=ALU.add).then_inc(g_chain, 1)
                dve.wait_ge(g_chain, base + 6)
                dve.wait_ge(g_exp, t + 1)
                dve.tensor_tensor(gw[:, :], sel[:, :], gex[:, :], ALU.mult).then_inc(gw_done, 1)
                dve.wait_ge(gw_done, t + 1)
                dve.tensor_reduce(gsum[:, :], gw[:, :], AX.X, ALU.add).then_inc(gs_done, 1)
                dve.wait_ge(gs_done, t + 1)
                dve.reciprocal(grec[:, :], gsum[:, :]).then_inc(gr_done, 1)
                dve.wait_ge(gr_done, t + 1)
                dve.tensor_scalar(gate[:, p, :], gw[:, :], grec[:, 0:1], None, ALU.mult).then_inc(g_done, 1)

            def add_experts(t, p, half):
                dve.wait_ge(o_ps, 2 * t + half + 1)
                if half == 0:
                    dve.wait_ge(g_done, t + 1)
                    dve.wait_ge(x1t_sb, t + 1)
                    at_least(dve, out_done, 16 * (t - 1))
                for j in range(4):
                    e = 4 * half + j
                    if e:
                        dve.wait_ge(o_acc, NE * t + e)
                    dve.scalar_tensor_tensor(out=acc[:, p, :], in0=OUT[:, j * P:(j + 1) * P],
                                             scalar=gate[:, p, e:e + 1], in1=acc[:, p, :] if e else x1[:, p, :],
                                             op0=ALU.mult, op1=ALU.add).then_inc(o_acc, 1)

            def memory(t, p, s):
                n = STEPS * t + s
                dve.wait_ge(th_done, n + 1)
                dve.wait_ge(g_ps, n + 1)
                at_least(dve, tm_done, n)
                dve.tensor_tensor_scan(flat(mem[:, :, :]), flat(th[:, :, :]), MEM[:, 2 * s * B:2 * (s + 1) * B],
                                       0.0, ALU.mult, ALU.add).then_inc(m_done, 1)
                h = h2[:, p, s - 1, :, 1] if s else h2[:, 1 - p, STEPS - 1, :, 1]
                dve.wait_ge(to_done, n + 1)
                dve.tensor_scalar(wo[:, :, 0], to[:, :], -0.5, 0.5, ALU.mult, ALU.add).then_inc(w_done, 1)
                dve.wait_ge(w_done, n + 1)
                dve.scalar_tensor_tensor(out=wo[:, :, 1], in0=wo[:, :, 0], scalar=1.0, in1=h, op0=ALU.subtract,
                                         op1=ALU.mult, reverse0=True).then_inc(oh_done, 1)

            def new_h(t, p, s):
                n = STEPS * t + s
                dve.wait_ge(tm_done, n + 1)
                dve.wait_ge(oh_done, n + 1)
                if s == 0:
                    at_least(dve, l_ps, t - 1)
                    at_least(dve, hid_ps, 2 * (t - 1))
                dve.tensor_tensor_scan(flat(h2[:, p, s, :, :]), flat(tm[:, :, :]), flat(wo[:, :, :]), 0.0, ALU.mult,
                                       ALU.add).then_inc(h_done, 1)

            def iteration(t, p, has):
                q = 1 - p
                if has(0):
                    memory(t, p, 0)
                    new_h(t, p, 0)
                if has(-2):
                    add_experts(t - 2, p, 0)
                if has(3):
                    keys(t + 3, q)
                if has(0):
                    memory(t, p, 1)
                    new_h(t, p, 1)
                if has(3):
                    queries(t + 3, q)
                if has(1):
                    residual(t + 1, q)
                if has(2):
                    add_dims(t + 2)
                if has(0):
                    memory(t, p, 2)
                    new_h(t, p, 2)
                if has(4):
                    qk_ready(t + 4, p)
                if has(-2):
                    add_experts(t - 2, p, 1)
                if has(-1):
                    route(t - 1)
                if has(0):
                    memory(t, p, 3)
                    new_h(t, p, 3)
                if has(-1):
                    choose(t - 1, q)
                if has(3):
                    sum_heads(t + 3)

            pipeline(dve, iteration)


_INS = ["x", "cond_1024", "L0_cond_Wq", "L0_cond_bq", "L0_cond_Wk", "L0_cond_bk", "L0_cond_Wv", "L0_cond_bv",
        "L0_cond_Wo", "L0_cond_bo", "L0_attn_Wq", "L0_attn_Wk", "L0_attn_Wv", "L0_attn_Wo", "L0_attn_bo",
        "L0_cond2_w_W", "L0_cond2_w_b", "L0_cond2_wx_W", "L0_cond2_wx_b", "L0_cond2_wh_W", "L0_cond2_wh_b",
        "L0_ffn_router_w", "L0_ffn_w1_all", "L0_ffn_w2_all"]
_OUTS = [((B, S, C), "float32")]


def kernel(**inputs):
    import numpy as _np
    import concourse.bacc as _bacc
    from concourse import mybir as _mybir
    from concourse.bass_utils import run_bass_kernel_spmd as _run

    nc = _bacc.Bacc("TRN2", target_bir_lowering=False, num_devices=1)
    arrays, args = {}, []
    for name in _INS:
        a = _np.ascontiguousarray(inputs[name])
        arrays[f"in_{name}_dram"] = a
        args.append(nc.dram_tensor(f"in_{name}_dram", a.shape, _mybir.dt.from_np(a.dtype), kind="ExternalInput").ap())
    for i, (shape, dtype) in enumerate(_OUTS):
        dt = _mybir.dt.from_np(_np.dtype(dtype))
        args.append(nc.dram_tensor(f"out_{i}_dram", shape, dt, kind="ExternalOutput").ap())
    adaln_attention_recurrence_moe(nc, *args)
    r = _run(nc, [arrays], core_ids=[0])
    return r.results[0]["out_0_dram"]
```

```python
from contextlib import ExitStack

import concourse.bass as bass
from concourse import mybir

F32 = mybir.dt.float32
BF16 = mybir.dt.bfloat16
ALU = mybir.AluOpType
ACT = mybir.ActivationFunctionType
AX = mybir.AxisListType

B, S, C = 32, 128, 128
H, D = 16, 8
NE, DE = 8, 128
P = 128
STEPS = 4
TILES = S // STEPS
TOK = STEPS * B
GROUP = 4
PAIRS = B // 2
BODY = 4
LEAD, LAG = 4, 2
PEEL = 4
EPS = 1e-6
NONE = -3.0e38
SCALE = float(D) ** -0.5


def ds(start, size):
    return bass.ds(start, size)


def at_least(engine, semaphore, count):
    if not isinstance(count, int) or count > 0:
        engine.wait_ge(semaphore, count)


def pipeline(engine, iteration):
    for t in range(-LEAD, PEEL):
        iteration(t, t % 2, lambda off, t=t: 0 <= t + off < TILES)
    with engine.Fori(0, (TILES - LEAD - PEEL) // 2) as it:
        for k in range(2):
            iteration(2 * it + PEEL + k, k, lambda off: True)
    for t in range(TILES - LEAD, TILES + LAG):
        iteration(t, t % 2, lambda off, t=t: 0 <= t + off < TILES)


def adaln_attention_recurrence_moe(nc, x, cond, cWq, cbq, cWk, cbk, cWv, cbv, cWo, cbo, aWq, aWk, aWv, aWo, abo,
                                   w_W, w_b, wx_W, wx_b, wh_W, wh_b, router_w, w1_all, w2_all, out):
    with ExitStack() as ctx:
        def sb(name, shape, dt=F32):
            return ctx.enter_context(nc.sbuf_tensor(name, shape, dt))

        def sem(name):
            return ctx.enter_context(nc.semaphore(name))

        bank = [ctx.enter_context(nc.psum_tensor(f"bank{i}", [P, 512], F32)) for i in range(8)]

        ZH, ZO, MEM, TR, QKV, ATT, HID, OUT = bank

        ident = sb("ident", [P, P])
        cwq, cwk, cwv, cwo = (sb(n, [P, P]) for n in ("cwq", "cwk", "cwv", "cwo"))
        aw_raw = sb("aw_raw", [P, 3, P])
        aw = sb("aw", [P, 3, P])
        awo = sb("awo", [P, P])
        gwx = sb("gwx", [P, 2 * P])
        gwh = sb("gwh", [P, 2 * P])
        wxw, whw_raw, whw = sb("wxw", [P, P]), sb("whw_raw", [P, P]), sb("whw", [P, P])
        w1 = sb("w1", [P, NE, DE])
        w2 = sb("w2", [P, NE, C])
        rout_raw, routT = sb("rout_raw", [NE, P]), sb("routT", [P, NE])
        brow = sb("brow", [5, P])
        bcol = sb("bcol", [P, 5])
        grow = sb("grow", [1, 4 * P])
        gres = sb("gres", [1, 2, 4 * P])
        gpart = sb("gpart", [1, 3, 4 * P], BF16)
        gbias = sb("gbias", [3, 4 * P], BF16)
        ones = sb("ones", [3, 2 * TOK], BF16)
        scan_mask = sb("scan_mask", [P, D * D + D, H])
        cond_raw, condT = sb("cond_raw", [B, P]), sb("condT", [P, B])
        kvT = sb("kvT", [P, 2, B])
        m_head = sb("m_head", [P, H])
        m_dim = sb("m_dim", [P, D])
        m_hl = sb("m_hl", [P, D])
        rep_d = sb("rep_d", [P, P])
        rep_h = sb("rep_h", [P, P])
        kmask = sb("kmask", [P, H, B])
        vmask = sb("vmask", [P, D, B])
        kr = sb("kr", [P, H, B])
        vr = sb("vr", [P, D + 1, B])
        vbd = sb("vbd", [P, B, D + 1, D])
        xin = sb("xin", [P, 2, GROUP, P])
        XT = sb("XT", [P, B, S])
        CTX = sb("CTX", [P, S, B])
        qT = sb("qT", [P, 2, GROUP * P])
        kbd = sb("kbd", [P, 4, H, H])
        smax = sb("smax", [P, 2, 2 * H])
        ssub = sb("ssub", [P, 2, 2 * H, H])
        sexp = sb("sexp", [P, 2, 2 * H * H])
        pT = sb("pT", [P, 2, 2 * H * H])
        srec = sb("srec", [P, 2, 2, H])
        yT = sb("yT", [P, TOK])
        qkv = sb("qkv", [P, 2, 3, D, H])
        qmax = sb("qmax", [P, H])
        ex_in = sb("ex_in", [P, 2, D, H])
        ex = sb("ex", [P, 2, 2, D, H])
        qsum = sb("qsum", [P, H])
        kv = sb("kv", [P, D * D + D, H])
        kvs = sb("kvs", [P, D * D + D, H])
        den = sb("den", [P, D, H])
        rden = sb("rden", [P, D, H])
        qn = sb("qn", [P, 2, D, H])
        qc = sb("qc", [P, D, D, H])
        att = sb("att", [P, H, D])
        attT = sb("attT", [P, TOK])
        x1T = sb("x1T", [P, 2, STEPS, B])
        th = sb("th", [P, B, 2])
        to = sb("to", [P, B])
        mem = sb("mem", [P, B, 2])
        tm = sb("tm", [P, B, 2])
        wo = sb("wo", [P, B, 2])
        h2 = sb("h2", [P, 2, STEPS, B, 2])
        x1 = sb("x1", [P, TILES, C])
        lg = sb("lg", [P, 2, NE])
        top = sb("top", [P, 8])
        lead = sb("lead", [P, 8])
        dl, gex = sb("dl", [P, 2, NE]), sb("gex", [P, 2, NE])
        gw = sb("gw", [P, 2, NE])
        gw2, gsum, grec = sb("gw2", [P, NE]), sb("gsum", [P, 1]), sb("grec", [P, 2])
        hid = sb("hid", [P, 2, 4, DE])
        hsq = sb("hsq", [P, 2, 512])
        res = sb("res", [P, 2, C])

        x_in, w_in, w_late, gb_in, out_done = sem("x_in0"), sem("w_in"), sem("w_late"), sem("gb_in"), sem("out_done")
        x_in = [x_in, sem("x_in1")]
        consts, const_step, gsplit, ident_ok, m_dim_ok, res_done = (
            sem(n) for n in ("consts", "const_step", "gsplit", "ident_ok", "m_dim_ok", "res_done"))
        ct_ps, ct_sb, kv_ps, kv_sb, kvm, kvr_ps, kr_sb, vr_sb, vbd_ok, late_sb, h_init, rt_ps = (
            sem(n) for n in ("ct_ps", "ct_sb", "kv_ps", "kv_sb", "kvm", "kvr_ps", "kr_sb", "vr_sb", "vbd_ok",
                             "late_sb", "h_init", "rt_ps"))
        xT_ps, xT_sb, q_ps, q_sb = sem("xT_ps"), sem("xT_sb"), sem("q_ps"), sem("q_sb")
        kbd_ok, s_ps, s_max, s_sub, s_exp = sem("kbd_ok"), sem("s_ps"), sem("s_max"), sem("s_sub"), sem("s_exp")
        pT_ps, pT_sb, c_ps, c_rec, c_sb = sem("pT_ps"), sem("pT_sb"), sem("c_ps"), sem("c_rec"), sem("c_sb")
        y_ps, y_sb, qkv_ps, qkv_sb = sem("y_ps"), sem("y_sb"), sem("qkv_ps"), sem("qkv_sb")
        q_max, ex_ready, ex_done, k_ready, q_sum, k_sum = (
            sem(n) for n in ("q_max", "ex_ready", "ex_done", "k_ready", "q_sum", "k_sum"))
        kv_done, kv_sum, d_den, d_rec, qn_done, qc_done, a_red = (
            sem("kv_done"), sem("kv_sum"), sem("d_den"), sem("d_rec"), sem("qn_done"), sem("qc_done"), sem("a_red"))
        aT_ps, aT_sb, p_ps, x1_done, xz_done, x1t_ps, x1t_sb = (
            sem(n) for n in ("aT_ps", "aT_sb", "p_ps", "x1_done", "xz_done", "x1t_ps", "x1t_sb"))
        zh_ps, g_ps, zo_ps, th_done, to_done, m_done, w_done, oh_done, tm_done, h_done = (
            sem(n) for n in ("zh_ps", "g_ps", "zo_ps", "th_done", "to_done", "m_done", "w_done", "oh_done",
                             "tm_done", "h_done"))
        l_ps, l_sb, l_copy, l_lead, l_out, l_dl, g_exp, gw_done, g_sq, gs_done, gr_done = (
            sem(n) for n in ("l_ps", "l_sb", "l_copy", "l_lead", "l_out", "l_dl", "g_exp", "gw_done", "g_sq",
                             "gs_done", "gr_done"))
        hid_ps, hid_sb, hT_ps, hsq_sb, o_ps = sem("hid_ps"), sem("hid_sb"), sem("hT_ps"), sem("hsq_sb"), sem("o_ps")

        XTt = XT[:, :, :].rearrange("p b t -> p t b")
        CTXf = CTX[:, :, :].rearrange("p t b -> p (t b)")
        x_d = x.rearrange("(g j) s c -> g s j c", j=GROUP)
        out_d = out.rearrange("b (n l) c -> n l b c", l=STEPS)

        WEIGHTS = [(cond_raw[:, :], cond), (cwk[:, :], cWk), (cwv[:, :], cWv), (cwq[:, :], cWq)] + [
            (brow[i:i + 1, :], b.rearrange("(a n) -> a n", a=1)) for i, b in enumerate((cbq, cbk, cbv, cbo, abo))]
        LATE = [
            (cwo[:, :], cWo), (aw_raw[:, 0, :], aWq), (aw_raw[:, 1, :], aWk), (aw_raw[:, 2, :], aWv), (awo[:, :], aWo),
            (gwx[:, :], w_W[0:C, :]), (gwh[:, :], w_W[C:2 * C, :]), (wxw[:, :], wx_W), (whw_raw[:, :], wh_W),
            (grow[:, 0:2 * P], w_b.rearrange("(a n) -> a n", a=1)),
            (grow[:, 2 * P:3 * P], wx_b.rearrange("(a n) -> a n", a=1)),
            (grow[:, 3 * P:4 * P], wh_b.rearrange("(a n) -> a n", a=1)),
            (rout_raw[:, :], router_w),
            (w1[:, :, :], w1_all.rearrange("e c d -> c e d")), (w2[:, :, :], w2_all.rearrange("e d c -> d e c"))]
        W_ALL, LATE_ALL = 16 * len(WEIGHTS), 16 * len(LATE)

        block = ctx.enter_context(nc.Block())

        @block.sync
        def _(sp):
            def load_x(g, half):
                sp.dma_start(xin[:, half, :, :], x_d[g]).then_inc(x_in[half], 16)

            for dst, src in WEIGHTS[:2]:
                sp.dma_start(dst, src).then_inc(w_in, 16)
            for half in range(2):
                load_x(half, half)
            for dst, src in WEIGHTS[2:]:
                sp.dma_start(dst, src).then_inc(w_in, 16)
            for dst, src in LATE:
                sp.dma_start(dst, src).then_inc(w_late, 16)
            with sp.Fori(1, PAIRS // BODY) as it:
                for half in range(2):
                    sp.wait_ge(xT_ps, 2 * it + half - 1)
                    load_x(2 * it + half, half)
            sp.wait_ge(gsplit, 6)
            for i in range(3):
                sp.dma_start(gbias[i:i + 1, :], gpart[:, i, :]).then_inc(gb_in, 16)

            def store(t, p):
                at_least(sp, out_done, 16 * t)
                sp.wait_ge(res_done, NE * t + NE)
                sp.dma_start(out_d[t], res[:, p, :]).then_inc(out_done, 16)

            for t in range(2):
                store(t, t)
            with sp.Fori(1, TILES // 2) as it:
                for p in range(2):
                    store(2 * it + p, p)
            sp.wait_ge(out_done, 16 * TILES)

        @block.gpsimd
        def _(pool):
            n = [0]

            def link(ins):
                ins.then_inc(const_step, 1)
                n[0] += 1
                pool.wait_ge(const_step, n[0])

            def band(t, lo, hi, pattern, mult):
                link(pool.affine_select(out=t, in_=t, compare_op=ALU.is_ge, fill=0.0, base=-lo,
                                        pattern=pattern, channel_multiplier=mult))
                link(pool.affine_select(out=t, in_=t, compare_op=ALU.is_ge, fill=0.0, base=hi,
                                        pattern=[[-s, k] for s, k in pattern], channel_multiplier=-mult))

            link(pool.memset(ident[:, :], 1.0))
            band(ident[:, :], 0, 0, [[-1, P]], 1)
            pool.memset(vr[:, D, :], 1.0).then_inc(ident_ok, 1)
            link(pool.memset(m_head[:, :], 1.0))
            band(m_head[:, :], 0, D - 1, [[-D, H]], 1)
            link(pool.memset(m_hl[:, :], 1.0))
            band(m_hl[:, :], 0, H - 1, [[-H, D]], 1)
            pool.wait_ge(m_dim_ok, 1)
            link(pool.tensor_copy(rep_d[:, :].rearrange("p (h d) -> p h d", d=D),
                                  m_dim[:, :].unsqueeze(1).broadcast_to([P, H, D])))
            link(pool.tensor_copy(rep_h[:, :].rearrange("p (l h) -> p l h", h=H),
                                  m_head[:, :].unsqueeze(1).broadcast_to([P, D, H])))
            pool.memset(ones[:, :], 1.0).then_inc(consts, 1)

            def key_blocks(b, k):
                pool.tensor_tensor(kbd[:, k % 4, :, :], m_head[:, :].unsqueeze(2).broadcast_to([P, H, H]),
                                   kr[:, :, ds(b, 1)].rearrange("p h o -> p o h").broadcast_to([P, H, H]),
                                   ALU.mult).then_inc(kbd_ok, 1)

            pool.wait_ge(kr_sb, 1)
            for b in range(4):
                key_blocks(b, b)
            link(pool.memset(scan_mask[:, :, :], 1.0))
            pool.memset(scan_mask[:, :, 0:1], 0.0)
            pool.memset(lead[:, 2:], NONE)
            pool.memset(th[:, :, :], 0.0)
            pool.memset(tm[:, :, :], 0.0)
            pool.memset(h2[:, :, :, :, :], 0.0).then_inc(consts, 1)

            def key_pair(u, k):
                pool.wait_ge(s_ps, u - 1)
                for i in range(2):
                    key_blocks(2 * u + i, 2 * (k % 2) + i)

            with pool.Fori(0, PAIRS // BODY - 1) as it:
                for k in range(BODY):
                    key_pair(BODY * it + k + 2, k)
            for u in range(PAIRS - 2, PAIRS):
                key_pair(u, u)

            def split(ins):
                ins.then_inc(gsplit, 1)
                split.n += 1
                pool.wait_ge(gsplit, split.n)

            split.n = 0
            pool.wait_ge(w_late, LATE_ALL)
            split(pool.tensor_scalar(grow[:, 3 * P:], grow[:, 3 * P:], 0.5, None, ALU.mult))
            split(pool.tensor_copy(gpart[:, 0, :], grow[:, :]))
            split(pool.tensor_tensor(gres[:, 0, :], grow[:, :], gpart[:, 0, :], ALU.subtract))
            split(pool.tensor_copy(gpart[:, 1, :], gres[:, 0, :]))
            split(pool.tensor_tensor(gres[:, 1, :], gres[:, 0, :], gpart[:, 1, :], ALU.subtract))
            pool.tensor_copy(gpart[:, 2, :], gres[:, 1, :]).then_inc(gsplit, 1)

            def outer(t, p):
                pool.wait_ge(k_ready, t + 1)
                at_least(pool, kv_sum, 4 * t)
                pool.tensor_tensor(
                    kv[:, 0:D * D, :].rearrange("p (d e) h -> p d e h", d=D),
                    kv[:, D * D:, :].unsqueeze(2).broadcast_to([P, D, D, H]),
                    qkv[:, p, 2, :, :].unsqueeze(1).broadcast_to([P, D, D, H]), ALU.mult).then_inc(kv_done, 1)

            def weigh(t, p):
                pool.wait_ge(kv_sum, 4 * t + 4)
                pool.wait_ge(qn_done, t + 1)
                at_least(pool, a_red, 2 * t)
                pool.tensor_tensor(
                    qc[:, :, :, :], kvs[:, 0:D * D, :].rearrange("p (d e) h -> p d e h", d=D),
                    qn[:, p, :, :].unsqueeze(2).broadcast_to([P, D, D, H]), ALU.mult).then_inc(qc_done, 1)

            def iteration(t, p, has):
                if has(2):
                    weigh(t + 2, p)
                if has(3):
                    outer(t + 3, 1 - p)

            pipeline(pool, iteration)

        @block.tensor
        def _(pe):
            def mm(dst, w, rhs, start=True):
                return pe.matmul(dst, w, rhs, start=start, stop=True, skip_group_check=True)

            def x_T(g, half, it):
                pe.wait_ge(x_in[half], 16 * it + 16)
                at_least(pe, xT_sb, g)
                for j in range(GROUP):
                    last = pe.transpose(bank[6][:, j * P:(j + 1) * P], xin[:, half, j, :], ident[:, :])
                last.then_inc(xT_ps, 1)

            def q_of(g):
                pe.wait_ge(xT_sb, g + 1)
                at_least(pe, q_sb, g)
                mm(bank[7][:, :], cwq[:, :], XT[:, ds(GROUP * g, GROUP), :].rearrange("p b s -> p (b s)"))\
                    .then_inc(q_ps, 1)

            pe.wait_ge(ident_ok, 1)
            x_T(0, 0, 0)
            pe.wait_ge(w_in, W_ALL)
            pe.transpose(bank[0][:, 0:B], cond_raw[:, :], ident[0:B, 0:B])
            pe.transpose(bank[0][:, B:B + 5], brow[:, :], ident[0:5, 0:5]).then_inc(ct_ps, 1)
            pe.wait_ge(ct_sb, 2)
            mm(bank[1][:, 0:B], cwk[:, :], condT[:, :])
            mm(bank[1][:, B:2 * B], cwv[:, :], condT[:, :]).then_inc(kv_ps, 1)
            q_of(0)
            pe.wait_ge(consts, 1)
            pe.wait_ge(kvm, 2)
            mm(bank[2][:, :], rep_d[:, :], kmask[:, :, :].rearrange("p h b -> p (h b)"))
            mm(bank[3][:, 0:D * B], rep_h[:, :], vmask[:, :, :].rearrange("p d b -> p (d b)")).then_inc(kvr_ps, 1)

            def scores(u, k, g):
                if k % 2 == 0:
                    pe.wait_ge(q_sb, g + 1)
                pe.wait_ge(kbd_ok, 2 * u + 2)
                at_least(pe, s_sub, u - 1)
                for i in range(2):
                    j = 2 * (k % 2) + i
                    last = mm(bank[k % 2][:, i * H * H:(i + 1) * H * H], qT[:, k // 2, j * P:(j + 1) * P],
                              kbd[:, j, :, :].rearrange("p h g -> p (h g)"))
                last.then_inc(s_ps, 1)

            def probs_T(u, k):
                pe.wait_ge(s_exp, u + 1)
                at_least(pe, pT_sb, u - 1)
                for j in range(4):
                    last = pe.transpose(bank[2 + k % 2][:, j * P:(j + 1) * P], sexp[:, k % 2, j * P:(j + 1) * P],
                                        ident[:, :])
                last.then_inc(pT_ps, 1)

            def context(u, k):
                pe.wait_ge(pT_sb, u + 1)
                at_least(pe, c_sb, u - 1)
                if isinstance(u, int) and u == 0:
                    pe.wait_ge(vbd_ok, 1)
                for i in range(2):
                    dst = bank[4 + k % 2][:, i * 144:(i + 1) * 144].rearrange("p (d j l) -> p d j l", d=D + 1, j=2)
                    for j in range(2):
                        last = mm(dst[:, :, j, :], pT[:, k % 2, (2 * i + j) * P:(2 * i + j + 1) * P],
                                  vbd[:, ds(2 * u + i, 1), :, :].rearrange("p o d h -> p (o d) h"))
                last.then_inc(c_ps, 1)

            def first(it, start, end):
                for k in range(BODY):
                    u = BODY * it + k
                    ahead = k % 2 == 0 and not (end and k)
                    if ahead:
                        x_T(2 * it + k // 2 + 1, 1 - k // 2, it + k // 2)
                    if not (end and k == BODY - 1):
                        scores(u + 1, (k + 1) % BODY, 2 * it + (k + 1) // 2)
                    if ahead:
                        q_of(2 * it + k // 2 + 1)
                    probs_T(u, k)
                    if not (start and k == 0):
                        context(u - 1, (k - 1) % BODY)

            pe.wait_ge(kr_sb, 1)
            scores(0, 0, 0)
            first(0, True, False)
            with pe.Fori(1, PAIRS // BODY - 1) as it:
                first(it, False, False)
            first(PAIRS // BODY - 1, False, True)
            context(PAIRS - 1, BODY - 1)

            pe.wait_ge(w_late, LATE_ALL)
            pe.transpose(bank[6][:, 0:NE], rout_raw[:, :], ident[0:NE, 0:NE]).then_inc(rt_ps, 1)
            pe.wait_ge(late_sb, 3)
            pe.wait_ge(consts, 2)
            pe.wait_ge(h_init, 2)
            pe.wait_ge(c_sb, PAIRS)
            pe.wait_ge(gb_in, 48)

            def h_of(p):
                return h2[:, p, :, :, 1].rearrange("p l b -> p (l b)")

            def y(t):
                at_least(pe, qkv_sb, t)
                mm(QKV[:, 0:P], cwo[:, :], CTXf[:, ds(TOK * t, TOK)]).then_inc(y_ps, 1)

            def qkv_of(t):
                pe.wait_ge(y_sb, t + 1)
                mm(QKV[:, P:], yT[:, :], aw[:, :, :].rearrange("p w n -> p (w n)")).then_inc(qkv_ps, 1)

            def att_T(t):
                pe.wait_ge(a_red, 2 * t + 2)
                at_least(pe, x1_done, t)
                at_least(pe, x1t_sb, t)
                pe.transpose(ATT[:, 0:P], att[:, :, :].rearrange("p h e -> p (h e)"), ident[:, :]).then_inc(aT_ps, 1)

            def project_out(t):
                pe.wait_ge(aT_sb, t + 1)
                mm(ATT[:, P:2 * P], awo[:, :], attT[:, :]).then_inc(p_ps, 1)

            def x_rows(t, p):
                pe.wait_ge(x1_done, t + 1)
                pe.transpose(ATT[:, 2 * P:3 * P], x1T[:, p, :, :].rearrange("p l b -> p (l b)"), ident[:, :])\
                    .then_inc(x1t_ps, 1)

            def gates_x(t, p):
                xs = x1T[:, p, :, :].rearrange("p l b -> p (l b)")
                pe.wait_ge(x1_done, t + 1)
                at_least(pe, th_done, STEPS * t)
                mm(ZH[:, 0:TOK], gbias[:, 0:P], ones[:, 0:TOK])
                mm(ZH[:, 0:TOK], gwx[:, 0:P], xs, start=False)
                at_least(pe, to_done, STEPS * t)
                mm(ZO[:, 0:TOK], gbias[:, P:2 * P], ones[:, 0:TOK])
                mm(ZO[:, 0:TOK], gwx[:, P:2 * P], xs, start=False)

            def memory_x(t, p):
                xs = x1T[:, p, :, :].rearrange("p l b -> p (l b)")
                odd = MEM[:, 1:2 * TOK:2]
                at_least(pe, m_done, STEPS * t)
                mm(MEM[:, 0:2 * TOK], gbias[:, 3 * P:], ones[:, :])
                mm(odd, gbias[:, 2 * P:3 * P], ones[:, 0:TOK], start=False)
                mm(odd, wxw[:, :], xs, start=False).then_inc(xz_done, 1)

            def logits(t, p, last):
                pe.wait_ge(h_done, STEPS * t + STEPS)
                mm(MEM[:, 2 * TOK:2 * TOK + NE], h_of(p), routT[:, :], start=last).then_inc(l_ps, 1)

            def hidden(t, p, half):
                pe.wait_ge(h_done, STEPS * t + STEPS)
                at_least(pe, hid_sb, 2 * t + half)
                mm(HID[:, :], h_of(p), w1[:, 4 * half:4 * half + 4, :].rearrange("p e d -> p (e d)"))\
                    .then_inc(hid_ps, 1)

            def hidden_T(t, half):
                pe.wait_ge(hid_sb, 2 * t + half + 1)
                at_least(pe, hsq_sb, 2 * t + half)
                for j in range(4):
                    last = pe.transpose(TR[:, j * P:(j + 1) * P], hid[:, half, j, :], ident[:, :])
                last.then_inc(hT_ps, 1)

            def experts_out(t, half):
                pe.wait_ge(hsq_sb, 2 * t + half + 1)
                if half == 0:
                    at_least(pe, res_done, NE * t)
                for j in range(4):
                    last = mm(OUT[:, 0:C], hsq[:, half, j * P:(j + 1) * P], w2[:, 4 * half + j, :],
                              start=half == 0 and j == 0)
                last.then_inc(o_ps, 1)

            def step(t, p, s, before_memory=None):
                at_least(pe, h_done, STEPS * t + s)
                h = h2[:, p, s - 1, :, 1] if s else h2[:, 1 - p, STEPS - 1, :, 1]
                col = s * B
                mm(ZH[:, col:col + B], gwh[:, 0:P], h, start=False).then_inc(zh_ps, 1)
                if before_memory:
                    before_memory()
                mm(MEM[:, 2 * s * B:2 * (s + 1) * B], whw[:, :], h.unsqueeze(2).broadcast_to([P, B, 2]),
                   start=False).then_inc(g_ps, 1)
                mm(ZO[:, col:col + B], gwh[:, P:2 * P], h, start=False).then_inc(zo_ps, 1)

            def iteration(t, p, has):
                q = 1 - p
                if has(0):
                    step(t, p, 0, (lambda: logits(t - 1, q, False)) if has(-1) else None)
                elif has(-1):
                    logits(t - 1, q, True)
                if has(1):
                    att_T(t + 1)
                if has(-2):
                    experts_out(t - 2, 0)
                if has(4):
                    y(t + 4)
                if has(1):
                    project_out(t + 1)
                if has(0):
                    step(t, p, 1)
                if has(-2):
                    hidden_T(t - 2, 1)
                if has(-1):
                    hidden(t - 1, q, 0)
                if has(0):
                    step(t, p, 2)
                if has(4):
                    qkv_of(t + 4)
                if has(1):
                    x_rows(t + 1, q)
                if has(-2):
                    experts_out(t - 2, 1)
                if has(0):
                    step(t, p, 3)
                if has(-1):
                    hidden_T(t - 1, 0)
                    hidden(t - 1, q, 1)
                if has(1):
                    gates_x(t + 1, q)
                    memory_x(t + 1, q)

            pipeline(pe, iteration)

        @block.scalar
        def _(act):
            act.preload_act_table(ACT.Exp)
            def group_T(g):
                act.wait_ge(xT_ps, g + 1)
                act.activation(XT[:, ds(GROUP * g, GROUP), :].rearrange("p b s -> p (b s)"), bank[6][:, :], ACT.Copy)\
                    .then_inc(xT_sb, 1)

            def group_q(g, half):
                act.wait_ge(q_ps, g + 1)
                at_least(act, s_ps, 2 * (g - 1))
                act.activation(qT[:, half, :], bank[7][:, :], ACT.Identity, bias=bcol[:, 0:1]).then_inc(q_sb, 1)

            def exps(u, k):
                act.wait_ge(s_sub, u + 1)
                at_least(act, pT_ps, u - 1)
                act.activation(sexp[:, k % 2, :], ssub[:, k % 2, :, :].rearrange("p h g -> p (h g)"), ACT.Exp,
                               scale=SCALE).then_inc(s_exp, 1)

            def probs_out(u, k):
                act.wait_ge(pT_ps, u + 1)
                at_least(act, c_ps, u - 1)
                act.activation(pT[:, k % 2, :], bank[2 + k % 2][:, :], ACT.Copy).then_inc(pT_sb, 1)

            def first(it, end):
                for k in range(BODY):
                    ahead = k % 2 == 0 and not (end and k)
                    if ahead:
                        group_T(2 * it + k // 2 + 1)
                    exps(BODY * it + k, k)
                    if ahead:
                        group_q(2 * it + k // 2 + 1, 1 - k // 2)
                    probs_out(BODY * it + k, k)

            group_T(0)
            act.wait_ge(ct_ps, 1)
            act.activation(condT[:, :], bank[0][:, 0:B], ACT.Copy).then_inc(ct_sb, 1)
            act.activation(bcol[:, :], bank[0][:, B:B + 5], ACT.Copy).then_inc(ct_sb, 1)
            act.wait_ge(kv_ps, 1)
            act.wait_ge(ct_sb, 2)
            for i in range(2):
                act.activation(kvT[:, i, :], bank[1][:, i * B:(i + 1) * B], ACT.Identity, bias=bcol[:, i + 1:i + 2])\
                    .then_inc(kv_sb, 1)
            group_q(0, 0)
            act.wait_ge(kvr_ps, 1)
            act.activation(kr[:, :, :].rearrange("p h b -> p (h b)"), bank[2][:, :], ACT.Copy).then_inc(kr_sb, 1)
            act.activation(vr[:, 0:D, :].rearrange("p d b -> p (d b)"), bank[3][:, 0:D * B], ACT.Copy)\
                .then_inc(vr_sb, 1)
            first(0, False)
            with act.Fori(1, PAIRS // BODY - 1) as it:
                first(it, False)
            first(PAIRS // BODY - 1, True)

            act.wait_ge(w_late, LATE_ALL)
            for w in range(2):
                act.activation(aw[:, w, :].rearrange("p (d h) -> p d h", d=D),
                               aw_raw[:, w, :].rearrange("p (h d) -> p d h", d=D), ACT.Copy)
            act.activation(aw[:, 2, :].rearrange("p (d h) -> p d h", d=D),
                           aw_raw[:, 2, :].rearrange("p (h d) -> p d h", d=D), ACT.Copy).then_inc(late_sb, 2)
            act.wait_ge(rt_ps, 1)
            act.activation(routT[:, :], bank[6][:, 0:NE], ACT.Copy).then_inc(late_sb, 1)

            def y_out(t):
                act.wait_ge(y_ps, t + 1)
                at_least(act, qkv_ps, t)
                act.activation(yT[:, :], QKV[:, 0:P], ACT.Identity, bias=bcol[:, 3:4]).then_inc(y_sb, 1)

            def qkv_out(t, p):
                act.wait_ge(qkv_ps, t + 1)
                at_least(act, kv_done, t - 1)
                act.activation(qkv[:, p, :, :, :].rearrange("p w d h -> p (w d h)"), QKV[:, P:], ACT.Copy)\
                    .then_inc(qkv_sb, 1)

            def exp_qk(t, p):
                act.wait_ge(ex_ready, t + 1)
                at_least(act, qn_done, t - 1)
                act.activation(ex[:, p, :, :, :].rearrange("p w d h -> p (w d h)"),
                               ex_in[:, :, :, :].rearrange("p w d h -> p (w d h)"), ACT.Exp).then_inc(ex_done, 1)

            def att_out(t):
                act.wait_ge(aT_ps, t + 1)
                at_least(act, p_ps, t)
                act.activation(attT[:, :], ATT[:, 0:P], ACT.Copy).then_inc(aT_sb, 1)

            def x_rows_out(t):
                act.wait_ge(x1t_ps, t + 1)
                act.activation(x1[:, ds(t, 1), :].rearrange("p o c -> p (o c)"), ATT[:, 2 * P:3 * P], ACT.Copy)\
                    .then_inc(x1t_sb, 1)

            def relu(t, p, half, some):
                if some == 0:
                    act.wait_ge(hid_ps, 2 * t + half + 1)
                    act.wait_ge(gw_done, t + 1)
                    at_least(act, hT_ps, 2 * t + half - 1)
                for j in range(2 * some, 2 * some + 2):
                    e = 4 * half + j
                    last = act.activation(hid[:, half, j, :], HID[:, j * DE:(j + 1) * DE], ACT.Relu,
                                          scale=gw[:, p, e:e + 1])
                if some:
                    last.then_inc(hid_sb, 1)

            def square(t, half):
                act.wait_ge(hT_ps, 2 * t + half + 1)
                at_least(act, o_ps, 2 * t + half - 1)
                act.activation(hsq[:, half, :], TR[:, :], ACT.Square).then_inc(hsq_sb, 1)

            def gate_exp(t):
                act.wait_ge(l_dl, t + 1)
                at_least(act, gw_done, t)
                act.activation(gex[:, :, :], dl[:, :, :], ACT.Exp, scale=0.5).then_inc(g_exp, 1)

            def gates(t, p, s):
                n = STEPS * t + s
                col = s * B
                act.wait_ge(zh_ps, n + 1)
                at_least(act, m_done, n)
                act.activation(th[:, :, 1], ZH[:, col:col + B], ACT.Tanh, scale=0.5).then_inc(th_done, 1)
                act.wait_ge(zo_ps, n + 1)
                at_least(act, w_done, n)
                act.activation(to[:, :], ZO[:, col:col + B], ACT.Tanh, scale=0.5)\
                    .then_inc(to_done, 1)

            def memory_tanh(t, s):
                n = STEPS * t + s
                act.wait_ge(m_done, n + 1)
                at_least(act, h_done, n)
                act.activation(tm[:, :, 1], mem[:, :, 1], ACT.Tanh).then_inc(tm_done, 1)

            def iteration(t, p, has):
                q = 1 - p
                if has(0):
                    gates(t, p, 0)
                if has(-2):
                    relu(t - 2, p, 1, 0)
                if has(0):
                    memory_tanh(t, 0)
                if has(1):
                    att_out(t + 1)
                if has(-2):
                    relu(t - 2, p, 1, 1)
                if has(4):
                    y_out(t + 4)
                if has(0):
                    gates(t, p, 1)
                if has(-1):
                    gate_exp(t - 1)
                if has(0):
                    memory_tanh(t, 1)
                if has(3):
                    exp_qk(t + 3, q)
                if has(-2):
                    square(t - 2, 1)
                if has(0):
                    gates(t, p, 2)
                if has(-1):
                    relu(t - 1, q, 0, 0)
                if has(0):
                    memory_tanh(t, 2)
                if has(-1):
                    relu(t - 1, q, 0, 1)
                if has(0):
                    gates(t, p, 3)
                if has(1):
                    x_rows_out(t + 1)
                if has(0):
                    memory_tanh(t, 3)
                if has(4):
                    qkv_out(t + 4, p)
                if has(-1):
                    square(t - 1, 0)

            pipeline(act, iteration)

        @block.vector
        def _(dve):
            dve.wait_ge(ident_ok, 1)
            dve.tensor_reduce(m_dim[:, :], ident[:, :].rearrange("p (h d) -> p d h", d=D), AX.X, ALU.add)\
                .then_inc(m_dim_ok, 1)
            dve.wait_ge(consts, 1)
            dve.wait_ge(kv_sb, 2)
            dve.tensor_tensor(kmask[:, :, :], m_head[:, :].unsqueeze(2).broadcast_to([P, H, B]),
                              kvT[:, 0, :].unsqueeze(1).broadcast_to([P, H, B]), ALU.mult).then_inc(kvm, 1)
            dve.tensor_tensor(vmask[:, :, :], m_dim[:, :].unsqueeze(2).broadcast_to([P, D, B]),
                              kvT[:, 1, :].unsqueeze(1).broadcast_to([P, D, B]), ALU.mult).then_inc(kvm, 1)

            def largest(u, k):
                dve.wait_ge(s_ps, u + 1)
                dve.tensor_reduce(smax[:, k % 2, :], bank[k % 2][:, :].rearrange("p (h g) -> p h g", g=H), AX.X,
                                  ALU.max).then_inc(s_max, 1)

            def less_largest(u, k):
                dve.wait_ge(s_max, u + 1)
                at_least(dve, s_exp, u - 1)
                dve.tensor_tensor(ssub[:, k % 2, :, :], bank[k % 2][:, :].rearrange("p (h g) -> p h g", g=H),
                                  smax[:, k % 2, :].unsqueeze(2).broadcast_to([P, 2 * H, H]), ALU.subtract)\
                    .then_inc(s_sub, 1)

            def context_of(k):
                return bank[4 + k % 2][:, 0:288].rearrange("p (i d h) -> p i d h", i=2, d=D + 1)

            def inverse_sum(u, k):
                dve.wait_ge(c_ps, u + 1)
                dve.reciprocal(srec[:, k % 2, :, :], context_of(k)[:, :, D, :]).then_inc(c_rec, 1)

            def normalise(u, k):
                dve.wait_ge(c_rec, u + 1)
                dve.tensor_tensor(CTX[:, :, ds(2 * u, 2)].rearrange("p (d h) i -> p i d h", d=D),
                                  context_of(k)[:, :, 0:D, :],
                                  srec[:, k % 2, :, :].unsqueeze(2).broadcast_to([P, 2, D, H]), ALU.mult)\
                    .then_inc(c_sb, 1)

            def first(it, start, end):
                for k in range(BODY):
                    u = BODY * it + k
                    more, before = not (end and k == BODY - 1), not (start and k == 0)
                    if more:
                        largest(u + 1, k + 1)
                    if before:
                        inverse_sum(u - 1, k - 1)
                    if more:
                        less_largest(u + 1, k + 1)
                    if before:
                        normalise(u - 1, k - 1)

            largest(0, 0)
            less_largest(0, 0)
            dve.wait_ge(vr_sb, 1)
            dve.tensor_tensor(vbd[:, :, :, :], vr[:, :, :].rearrange("p d b -> p b d").unsqueeze(3)
                              .broadcast_to([P, B, D + 1, D]),
                              m_hl[:, :].unsqueeze(1).unsqueeze(1).broadcast_to([P, B, D + 1, D]), ALU.mult)\
                .then_inc(vbd_ok, 1)
            first(0, True, False)
            with dve.Fori(1, PAIRS // BODY - 1) as it:
                first(it, False, False)
            first(PAIRS // BODY - 1, False, True)
            inverse_sum(PAIRS - 1, BODY - 1)
            normalise(PAIRS - 1, BODY - 1)
            dve.wait_ge(consts, 2)
            dve.wait_ge(w_late, LATE_ALL)
            dve.tensor_scalar(whw[:, :], whw_raw[:, :], 0.5, None, ALU.mult).then_inc(h_init, 1)
            dve.tensor_copy(h2[:, 1, STEPS - 1, :, 1], condT[:, :]).then_inc(h_init, 1)

            def flat(ap):
                return ap.rearrange("p a b -> p (a b)")

            def head_max(t, p):
                dve.wait_ge(qkv_sb, t + 1)
                dve.tensor_reduce(qmax[:, :], qkv[:, p, 0, :, :].rearrange("p d h -> p h d"), AX.X, ALU.max)\
                    .then_inc(q_max, 1)

            def negative_keys(t, p):
                dve.wait_ge(qkv_sb, t + 1)
                at_least(dve, ex_done, t)
                dve.tensor_scalar(ex_in[:, 1, :, :], qkv[:, p, 1, :, :], 0.0, None, ALU.min)

            def less_max(t, p):
                dve.wait_ge(q_max, t + 1)
                dve.tensor_tensor(ex_in[:, 0, :, :], qkv[:, p, 0, :, :],
                                  qmax[:, :].unsqueeze(1).broadcast_to([P, D, H]), ALU.subtract).then_inc(ex_ready, 1)

            def keys(t, p):
                dve.wait_ge(ex_done, t + 1)
                at_least(dve, kv_done, t)
                dve.scalar_tensor_tensor(out=kv[:, D * D:, :], in0=qkv[:, p, 1, :, :], scalar=0.0,
                                         in1=ex[:, p, 1, :, :], op0=ALU.max, op1=ALU.add).then_inc(k_ready, 1)
                dve.tensor_reduce(qsum[:, :], ex[:, p, 0, :, :].rearrange("p d h -> p h d"), AX.X, ALU.add)\
                    .then_inc(q_sum, 1)

            def key_sums(t):
                dve.wait_ge(k_ready, t + 1)
                dve.tensor_tensor_scan(flat(kvs[:, D * D:, :]), flat(scan_mask[:, D * D:, :]), flat(kv[:, D * D:, :]),
                                       0.0, ALU.mult, ALU.add).then_inc(k_sum, 1)

            def divisors(t):
                dve.wait_ge(q_sum, t + 1)
                dve.wait_ge(k_sum, t + 1)
                dve.scalar_tensor_tensor(out=den[:, :, :], in0=kvs[:, D * D:, :], scalar=EPS,
                                         in1=qsum[:, :].unsqueeze(1).broadcast_to([P, D, H]), op0=ALU.add,
                                         op1=ALU.mult).then_inc(d_den, 1)

            def inverses(t):
                dve.wait_ge(d_den, t + 1)
                dve.reciprocal(rden[:, :, :], den[:, :, :]).then_inc(d_rec, 1)

            def queries(t, p):
                dve.wait_ge(d_rec, t + 1)
                at_least(dve, qc_done, t - 1)
                dve.tensor_tensor(qn[:, p, :, :], ex[:, p, 0, :, :], rden[:, :, :], ALU.mult).then_inc(qn_done, 1)

            def sum_heads(t, part):
                a, b = part * D * D // 4, (part + 1) * D * D // 4
                if part == 0:
                    dve.wait_ge(kv_done, t + 1)
                    at_least(dve, qc_done, t)
                dve.tensor_tensor_scan(flat(kvs[:, a:b, :]), flat(scan_mask[:, a:b, :]), flat(kv[:, a:b, :]), 0.0,
                                       ALU.mult, ALU.add).then_inc(kv_sum, 1)

            def add_dims(t, half):
                a, b = half * D // 2, (half + 1) * D // 2
                if half == 0:
                    dve.wait_ge(qc_done, t + 1)
                    at_least(dve, aT_ps, t)
                dve.tensor_reduce(att[:, :, a:b].rearrange("p h e -> p e h"),
                                  qc[:, :, a:b, :].rearrange("p d e h -> p e h d"), AX.X, ALU.add).then_inc(a_red, 1)

            def residual(t, p):
                dve.wait_ge(p_ps, t + 1)
                at_least(dve, x1t_ps, t - 1)
                at_least(dve, xz_done, t - 1)
                dve.scalar_tensor_tensor(out=x1T[:, p, :, :],
                                         in0=ATT[:, P:2 * P].rearrange("p (l b) -> p l b", b=B),
                                         scalar=bcol[:, 4:5], in1=XTt[:, ds(STEPS * t, STEPS), :],
                                         op0=ALU.add, op1=ALU.add).then_inc(x1_done, 1)

            def route(t):
                dve.wait_ge(l_ps, t + 1)
                dve.tensor_copy(lg[:, 0, :], MEM[:, 2 * TOK:2 * TOK + NE]).then_inc(l_copy, 1)
                dve.max(top[:, :], MEM[:, 2 * TOK:2 * TOK + NE]).then_inc(l_sb, 1)

            def two_largest(t):
                dve.wait_ge(l_sb, t + 1)
                dve.tensor_copy(lead[:, 0:2], top[:, 0:2]).then_inc(l_lead, 1)

            def take_out(t):
                dve.match_replace(lg[:, 1, :], lead[:, :], lg[:, 0, :], NONE).then_inc(l_out, 1)

            def less_top(t):
                dve.wait_ge(l_out, t + 1)
                at_least(dve, g_exp, t)
                dve.tensor_scalar(dl[:, :, :], lg[:, :, :], top[:, 0:1], None, ALU.subtract).then_inc(l_dl, 1)

            def taken(t, p):
                dve.wait_ge(g_exp, t + 1)
                at_least(dve, hid_sb, 2 * (t - 1))
                dve.tensor_tensor(gw[:, p, :], gex[:, 0, :], gex[:, 1, :], ALU.subtract).then_inc(gw_done, 1)

            def taken_square(t, p):
                dve.wait_ge(gw_done, t + 1)
                dve.tensor_tensor(gw2[:, :], gw[:, p, :], gw[:, p, :], ALU.mult).then_inc(g_sq, 1)

            def taken_sum(t):
                dve.wait_ge(g_sq, t + 1)
                dve.tensor_reduce(gsum[:, :], gw2[:, :], AX.X, ALU.add).then_inc(gs_done, 1)

            def taken_inverse(t, p):
                dve.wait_ge(gs_done, t + 1)
                dve.reciprocal(grec[:, p:p + 1], gsum[:, :]).then_inc(gr_done, 1)

            def finish(t, p):
                dve.wait_ge(o_ps, 2 * t + 2)
                dve.wait_ge(gr_done, t + 1)
                dve.wait_ge(x1t_sb, t + 1)
                at_least(dve, out_done, 16 * (t - 1))
                dve.scalar_tensor_tensor(out=res[:, p, :], in0=OUT[:, 0:C], scalar=grec[:, p:p + 1],
                                         in1=x1[:, ds(t, 1), :].rearrange("p o c -> p (o c)"), op0=ALU.mult,
                                         op1=ALU.add).then_inc(res_done, NE)

            def memory(t, p, s):
                n = STEPS * t + s
                dve.wait_ge(th_done, n + 1)
                dve.wait_ge(g_ps, n + 1)
                at_least(dve, tm_done, n)
                dve.tensor_tensor_scan(flat(mem[:, :, :]), flat(th[:, :, :]), MEM[:, 2 * s * B:2 * (s + 1) * B],
                                       0.0, ALU.mult, ALU.add).then_inc(m_done, 1)
                dve.wait_ge(to_done, n + 1)
                dve.tensor_scalar(wo[:, :, 0], to[:, :], -0.5, 0.5, ALU.mult, ALU.add).then_inc(w_done, 1)

            def kept(t, p, s):
                n = STEPS * t + s
                h = h2[:, p, s - 1, :, 1] if s else h2[:, 1 - p, STEPS - 1, :, 1]
                dve.wait_ge(w_done, n + 1)
                dve.scalar_tensor_tensor(out=wo[:, :, 1], in0=wo[:, :, 0], scalar=1.0, in1=h, op0=ALU.subtract,
                                         op1=ALU.mult, reverse0=True).then_inc(oh_done, 1)

            def new_h(t, p, s):
                n = STEPS * t + s
                dve.wait_ge(tm_done, n + 1)
                dve.wait_ge(oh_done, n + 1)
                if s == 0:
                    at_least(dve, hid_ps, 2 * (t - 1))
                dve.tensor_tensor_scan(flat(h2[:, p, s, :, :]), flat(tm[:, :, :]), flat(wo[:, :, :]), 0.0, ALU.mult,
                                       ALU.add).then_inc(h_done, 1)

            def iteration(t, p, has):
                q = 1 - p
                if has(0):
                    memory(t, p, 0)
                if has(-1):
                    route(t - 1)
                if has(0):
                    kept(t, p, 0)
                if has(3):
                    head_max(t + 3, q)
                if has(-1):
                    two_largest(t - 1)
                if has(0):
                    new_h(t, p, 0)
                if has(-1):
                    dve.wait_ge(l_lead, t)
                    dve.wait_ge(l_copy, t)
                if has(3):
                    negative_keys(t + 3, q)
                elif has(-1):
                    dve.tensor_copy(gsum[:, :], lead[:, 0:1])
                if has(-1):
                    take_out(t - 1)
                if has(3):
                    less_max(t + 3, q)
                if has(-1):
                    less_top(t - 1)
                if has(2):
                    sum_heads(t + 2, 0)
                    sum_heads(t + 2, 1)
                if has(0):
                    memory(t, p, 1)
                if has(2):
                    sum_heads(t + 2, 2)
                if has(0):
                    kept(t, p, 1)
                if has(1):
                    residual(t + 1, q)
                if has(0):
                    new_h(t, p, 1)
                if has(2):
                    sum_heads(t + 2, 3)
                if has(-1):
                    taken(t - 1, q)
                if has(3):
                    keys(t + 3, q)
                if has(-1):
                    taken_square(t - 1, q)
                if has(0):
                    memory(t, p, 2)
                if has(3):
                    key_sums(t + 3)
                if has(0):
                    kept(t, p, 2)
                if has(-1):
                    taken_sum(t - 1)
                if has(3):
                    divisors(t + 3)
                if has(-1):
                    taken_inverse(t - 1, q)
                if has(0):
                    new_h(t, p, 2)
                if has(3):
                    inverses(t + 3)
                if has(0):
                    memory(t, p, 3)
                if has(-2):
                    finish(t - 2, p)
                if has(0):
                    kept(t, p, 3)
                if has(3):
                    queries(t + 3, q)
                if has(0):
                    new_h(t, p, 3)
                if has(2):
                    add_dims(t + 2, 0)
                    add_dims(t + 2, 1)

            pipeline(dve, iteration)


_INS = ["x", "cond_1024", "L0_cond_Wq", "L0_cond_bq", "L0_cond_Wk", "L0_cond_bk", "L0_cond_Wv", "L0_cond_bv",
        "L0_cond_Wo", "L0_cond_bo", "L0_attn_Wq", "L0_attn_Wk", "L0_attn_Wv", "L0_attn_Wo", "L0_attn_bo",
        "L0_cond2_w_W", "L0_cond2_w_b", "L0_cond2_wx_W", "L0_cond2_wx_b", "L0_cond2_wh_W", "L0_cond2_wh_b",
        "L0_ffn_router_w", "L0_ffn_w1_all", "L0_ffn_w2_all"]
_OUTS = [((B, S, C), "float32")]


def kernel(**inputs):
    import numpy as _np
    import concourse.bacc as _bacc
    from concourse import mybir as _mybir
    from concourse.bass_utils import run_bass_kernel_spmd as _run

    nc = _bacc.Bacc("TRN2", target_bir_lowering=False, num_devices=1)
    arrays, args = {}, []
    for name in _INS:
        a = _np.ascontiguousarray(inputs[name])
        arrays[f"in_{name}_dram"] = a
        args.append(nc.dram_tensor(f"in_{name}_dram", a.shape, _mybir.dt.from_np(a.dtype), kind="ExternalInput").ap())
    for i, (shape, dtype) in enumerate(_OUTS):
        dt = _mybir.dt.from_np(_np.dtype(dtype))
        args.append(nc.dram_tensor(f"out_{i}_dram", shape, dt, kind="ExternalOutput").ap())
    adaln_attention_recurrence_moe(nc, *args)
    r = _run(nc, [arrays], core_ids=[0])
    return r.results[0]["out_0_dram"]
```

```python
from contextlib import ExitStack

import concourse.bass as bass
from concourse import mybir

F32 = mybir.dt.float32
BF16 = mybir.dt.bfloat16
ALU = mybir.AluOpType
ACT = mybir.ActivationFunctionType
AX = mybir.AxisListType

B, S, C = 32, 128, 128
H, D = 16, 8
NE, DE = 8, 128
P = 128
STEPS = 4
TILES = S // STEPS
TOK = STEPS * B
GROUP = 4
EARLY = 4
PAIRS = B // 2
BODY = 4
LEAD, LAG = 4, 2
PEEL = 4
UNROLL = 4
EPS = 1e-6
NONE = -3.0e38
SCALE = float(D) ** -0.5


def ds(start, size):
    return bass.ds(start, size)


def at_least(engine, semaphore, count):
    if not isinstance(count, int) or count > 0:
        engine.wait_ge(semaphore, count)


def pipeline(engine, iteration):
    for t in range(-LEAD, PEEL):
        iteration(t, t % 2, lambda off, t=t: 0 <= t + off < TILES)
    with engine.Fori(0, (TILES - LEAD - PEEL) // UNROLL) as it:
        for k in range(UNROLL):
            iteration(UNROLL * it + PEEL + k, k % 2, lambda off: True)
    for t in range(TILES - LEAD, TILES + LAG):
        iteration(t, t % 2, lambda off, t=t: 0 <= t + off < TILES)


def adaln_attention_recurrence_moe(nc, x, cond, cWq, cbq, cWk, cbk, cWv, cbv, cWo, cbo, aWq, aWk, aWv, aWo, abo,
                                   w_W, w_b, wx_W, wx_b, wh_W, wh_b, router_w, w1_all, w2_all, out):
    with ExitStack() as ctx:
        def sb(name, shape, dt=F32):
            return ctx.enter_context(nc.sbuf_tensor(name, shape, dt))

        def sem(name):
            return ctx.enter_context(nc.semaphore(name))

        bank = [ctx.enter_context(nc.psum_tensor(f"bank{i}", [P, 512], F32)) for i in range(8)]

        ZH, ZO, MEM, TR, QKV, ATT, HID, OUT = bank

        ident = sb("ident", [P, P])
        cwq, cwk, cwv, cwo = (sb(n, [P, P]) for n in ("cwq", "cwk", "cwv", "cwo"))
        aw_raw = sb("aw_raw", [P, 3, P])
        aw = sb("aw", [P, 3, P])
        awo = sb("awo", [P, P])
        gwx = sb("gwx", [P, 2 * P])
        gwh = sb("gwh", [P, 2 * P])
        wxw, whw_raw, whw = sb("wxw", [P, P]), sb("whw_raw", [P, P]), sb("whw", [P, P])
        w1 = sb("w1", [P, NE, DE])
        w2 = sb("w2", [P, NE, C])
        rout_raw, routT = sb("rout_raw", [NE, P]), sb("routT", [P, NE])
        brow_kv, brow_q, brow_o = sb("brow_kv", [2, P]), sb("brow_q", [1, P]), sb("brow_o", [3, P])
        bcol = sb("bcol", [P, 5])
        gcol = sb("gcol", [P, 1])
        grow = sb("grow", [1, 3 * P])
        gres = sb("gres", [1, 2, 3 * P])
        gpart = sb("gpart", [1, 3, 3 * P], BF16)
        hbias = sb("hbias", [3, P], BF16)
        mbias = sb("mbias", [6, P], BF16)
        ones = sb("ones", [3, TOK], BF16)
        pairs = sb("pairs", [6, TOK, 2], BF16)
        scan_mask = sb("scan_mask", [P, D * D + D, H])
        cond_raw, condT = sb("cond_raw", [B, P]), sb("condT", [P, B])
        kvT = sb("kvT", [P, 2, B])
        m_head = sb("m_head", [P, H])
        m_dim = sb("m_dim", [P, D])
        m_hl = sb("m_hl", [P, D])
        rep_d = sb("rep_d", [P, P])
        rep_h = sb("rep_h", [P, P])
        kmask = sb("kmask", [P, H, B])
        vmask = sb("vmask", [P, D, B])
        kr = sb("kr", [P, H, B])
        vr = sb("vr", [P, D + 1, B])
        vbd = sb("vbd", [P, B, D + 1, D])
        xin = sb("xin", [P, 2, GROUP, P])
        XT = sb("XT", [P, B, S])
        CTX = sb("CTX", [P, S, B])
        qT = sb("qT", [P, 2, GROUP * P])
        kbd = sb("kbd", [P, 4, H, H])
        smax = sb("smax", [P, 2, 2 * H])
        ssub = sb("ssub", [P, 2, 2 * H, H])
        sexp = sb("sexp", [P, 2, 2 * H * H])
        pT = sb("pT", [P, 2, 2 * H * H])
        srec = sb("srec", [P, 2, 2, H])
        yT = sb("yT", [P, TOK])
        qkv = sb("qkv", [P, 2, 3, D, H])
        qmax = sb("qmax", [P, H])
        ex_in = sb("ex_in", [P, D, H])
        nk = sb("nk", [P, 2, D, H])
        ex = sb("ex", [P, 2, 2, D, H])
        qsum = sb("qsum", [P, H])
        kv = sb("kv", [P, D * D + D, H])
        kvs = sb("kvs", [P, D * D + D, H])
        den = sb("den", [P, D, H])
        rden = sb("rden", [P, D, H])
        qn = sb("qn", [P, 2, D, H])
        qc = sb("qc", [P, D, D, H])
        att = sb("att", [P, H, D])
        attT = sb("attT", [P, TOK])
        x1T = sb("x1T", [P, 2, STEPS, B])
        th = sb("th", [P, B, 2])
        to = sb("to", [P, B])
        mem = sb("mem", [P, B, 2])
        tm = sb("tm", [P, B, 2])
        wo = sb("wo", [P, B, 2])
        h2 = sb("h2", [P, 2, STEPS, B, 2])
        x1 = sb("x1", [P, TILES, C])
        lg = sb("lg", [P, 2, NE])
        top = sb("top", [P, 8])
        lead = sb("lead", [P, 8])
        dl, gex = sb("dl", [P, 2, NE]), sb("gex", [P, 2, NE])
        gw = sb("gw", [P, 2, NE])
        gw2, gsum, grec = sb("gw2", [P, NE]), sb("gsum", [P, 1]), sb("grec", [P, 2])
        hid = sb("hid", [P, 2, 4, DE])
        hsq = sb("hsq", [P, 2, 512])
        res = sb("res", [P, 2, C])

        w_kv, w_q, w_late, gb_in, out_done = (sem(n) for n in ("w_kv", "w_q", "w_late", "gb_in", "out_done"))
        x_in = [sem("x_in0"), sem("x_in1")]
        consts, const_step, gsplit, ident_ok, m_dim_ok, res_done = (
            sem(n) for n in ("consts", "const_step", "gsplit", "ident_ok", "m_dim_ok", "res_done"))
        ct_ps, ct_sb, kv_ps, kv_sb, kvm, kr_ps, vr_ps, kr_sb, vr_sb, vbd_ok, bq_ps, bq_sb = (
            sem(n) for n in ("ct_ps", "ct_sb", "kv_ps", "kv_sb", "kvm", "kr_ps", "vr_ps", "kr_sb", "vr_sb", "vbd_ok",
                             "bq_ps", "bq_sb"))
        kbd0_ok, aw_ok, h_init, rt_ps, rt_sb = (sem(n) for n in ("kbd0_ok", "aw_ok", "h_init", "rt_ps", "rt_sb"))
        xT_ps, xT_sb, q_ps, q_sb = sem("xT_ps"), sem("xT_sb"), sem("q_ps"), sem("q_sb")
        kbd_ok, s_ps, s_max, s_sub, s_exp = sem("kbd_ok"), sem("s_ps"), sem("s_max"), sem("s_sub"), sem("s_exp")
        pT_ps, pT_sb, c_ps, c_rec, c_sb = sem("pT_ps"), sem("pT_sb"), sem("c_ps"), sem("c_rec"), sem("c_sb")
        y_ps, y_sb, qkv_ps, qkv_sb = sem("y_ps"), sem("y_sb"), sem("qkv_ps"), sem("qkv_sb")
        nk_done = sem("nk_done")
        q_max, ex_ready, ex_done, k_ready, q_sum, k_sum = (
            sem(n) for n in ("q_max", "ex_ready", "ex_done", "k_ready", "q_sum", "k_sum"))
        kv_done, kv_sum, d_den, d_rec, qn_done, qc_done, a_red = (
            sem("kv_done"), sem("kv_sum"), sem("d_den"), sem("d_rec"), sem("qn_done"), sem("qc_done"), sem("a_red"))
        aT_ps, aT_sb, p_ps, x1_done, xz_done, x1t_ps, x1t_sb = (
            sem(n) for n in ("aT_ps", "aT_sb", "p_ps", "x1_done", "xz_done", "x1t_ps", "x1t_sb"))
        zh_ps, g_ps, zo_ps, th_done, to_done, m_done, w_done, oh_done, tm_done, h_done = (
            sem(n) for n in ("zh_ps", "g_ps", "zo_ps", "th_done", "to_done", "m_done", "w_done", "oh_done",
                             "tm_done", "h_done"))
        l_ps, l_sb, l_copy, l_lead, l_out, l_dl, g_exp, gw_done, gs_done, gr_done = (
            sem(n) for n in ("l_ps", "l_sb", "l_copy", "l_lead", "l_out", "l_dl", "g_exp", "gw_done",
                             "gs_done", "gr_done"))
        hid_ps, hid_sb, hT_ps, hsq_sb, o_ps = sem("hid_ps"), sem("hid_sb"), sem("hT_ps"), sem("hsq_sb"), sem("o_ps")

        XTt = XT[:, :, :].rearrange("p b t -> p t b")
        CTXf = CTX[:, :, :].rearrange("p t b -> p (t b)")
        x_d = x.rearrange("(g j) s c -> g s j c", j=GROUP)
        out_d = out.rearrange("b (n l) c -> n l b c", l=STEPS)

        def row(b):
            return b.rearrange("(a n) -> a n", a=1)

        KV = [(cond_raw[:, :], cond), (cwk[:, :], cWk), (brow_kv[0:1, :], row(cbk)), (cwv[:, :], cWv),
              (brow_kv[1:2, :], row(cbv))]
        Q = [(cwq[:, :], cWq), (brow_q[:, :], row(cbq))]
        LATE = [
            (cwo[:, :], cWo), (aw_raw[:, 0, :], aWq), (aw_raw[:, 1, :], aWk), (aw_raw[:, 2, :], aWv), (awo[:, :], aWo),
            (gwx[:, :], w_W[0:C, :]), (gwh[:, :], w_W[C:2 * C, :]), (wxw[:, :], wx_W), (whw_raw[:, :], wh_W),
            (grow[:, 0:P], row(wx_b)), (grow[:, P:2 * P], row(wh_b)),
            (grow[:, 2 * P:], row(w_b[0:P])),
            (brow_o[0:1, :], row(cbo)), (brow_o[1:2, :], row(abo)), (brow_o[2:3, :], row(w_b[P:])),
            (rout_raw[:, :], router_w),
            (w1[:, :, :], w1_all.rearrange("e c d -> c e d")), (w2[:, :, :], w2_all.rearrange("e d c -> d e c"))]
        LATE_ALL = 16 * len(LATE)

        block = ctx.enter_context(nc.Block())

        keys_early = bank[4][:, 0:H * EARLY].rearrange("p (h b) -> p h b", h=H)
        keys_late = bank[5][:, 0:H * (B - EARLY)].rearrange("p (h b) -> p h b", h=H)

        def key_blocks(engine, b, k):
            return engine.tensor_tensor(kbd[:, k % 4, :, :], m_head[:, :].unsqueeze(2).broadcast_to([P, H, H]),
                                        kr[:, :, ds(b, 1)].rearrange("p h o -> p o h").broadcast_to([P, H, H]),
                                        ALU.mult)

        def is_last(t):
            return isinstance(t, int) and t == TILES - 1

        def hidden_bank(t, half):
            return (QKV, ATT)[half] if is_last(t) else HID

        def out_bank(t):
            return ZO if is_last(t) else OUT

        @block.sync
        def _(sp):
            def load_x(g, half):
                sp.dma_start(xin[:, half, :, :], x_d[g]).then_inc(x_in[half], 16)

            for dst, src in KV:
                sp.dma_start(dst, src).then_inc(w_kv, 16)
            load_x(0, 0)
            for dst, src in Q:
                sp.dma_start(dst, src).then_inc(w_q, 16)
            load_x(1, 1)
            for dst, src in LATE:
                sp.dma_start(dst, src).then_inc(w_late, 16)
            with sp.Fori(1, PAIRS // BODY) as it:
                for half in range(2):
                    sp.wait_ge(xT_ps, 2 * it + half - 1)
                    load_x(2 * it + half, half)
            sp.wait_ge(gsplit, 6)
            for i in range(3):
                sp.dma_start(mbias[i:i + 1, :], gpart[:, i, P:2 * P]).then_inc(gb_in, 16)
                sp.dma_start(mbias[3 + i:4 + i, :], gpart[:, i, 0:P]).then_inc(gb_in, 16)
                sp.dma_start(hbias[i:i + 1, :], gpart[:, i, 2 * P:]).then_inc(gb_in, 16)

            def store(t, p):
                at_least(sp, out_done, 16 * t)
                sp.wait_ge(res_done, NE * t + NE)
                sp.dma_start(out_d[t], res[:, p, :]).then_inc(out_done, 16)

            for t in range(2):
                store(t, t)
            with sp.Fori(1, TILES // 2) as it:
                for p in range(2):
                    store(2 * it + p, p)
            sp.wait_ge(out_done, 16 * TILES)

        @block.gpsimd
        def _(pool):
            n = [0]

            def link(ins):
                ins.then_inc(const_step, 1)
                n[0] += 1
                pool.wait_ge(const_step, n[0])

            def band(t, lo, hi, pattern, mult):
                link(pool.affine_select(out=t, in_=t, compare_op=ALU.is_ge, fill=0.0, base=-lo,
                                        pattern=pattern, channel_multiplier=mult))
                link(pool.affine_select(out=t, in_=t, compare_op=ALU.is_ge, fill=0.0, base=hi,
                                        pattern=[[-s, k] for s, k in pattern], channel_multiplier=-mult))

            link(pool.memset(ident[:, :], 1.0))
            band(ident[:, :], 0, 0, [[-1, P]], 1)
            pool.memset(vr[:, D, :], 1.0).then_inc(ident_ok, 1)
            link(pool.memset(m_head[:, :], 1.0))
            band(m_head[:, :], 0, D - 1, [[-D, H]], 1)
            link(pool.memset(m_hl[:, :], 1.0))
            band(m_hl[:, :], 0, H - 1, [[-H, D]], 1)
            pool.wait_ge(m_dim_ok, 1)
            link(pool.tensor_copy(rep_d[:, :].rearrange("p (h d) -> p h d", d=D),
                                  m_dim[:, :].unsqueeze(1).broadcast_to([P, H, D])))
            link(pool.tensor_copy(rep_h[:, :].rearrange("p (l h) -> p l h", h=H),
                                  m_head[:, :].unsqueeze(1).broadcast_to([P, D, H])))
            pool.memset(ones[:, :], 1.0).then_inc(consts, 1)

            pool.wait_ge(kr_sb, 1)
            for b in range(2, 4):
                key_blocks(pool, b, b).then_inc(kbd_ok, 1)
            link(pool.memset(scan_mask[:, :, :], 1.0))
            pool.memset(scan_mask[:, :, 0:1], 0.0)
            link(pool.memset(pairs[:, :, :], 1.0))
            link(pool.affine_select(out=pairs[:, :, 0], in_=pairs[:, :, 0], compare_op=ALU.is_ge, fill=0.0, base=2,
                                    pattern=[[0, TOK]], channel_multiplier=-1))
            pool.memset(lead[:, 2:], NONE)
            pool.memset(th[:, :, :], 0.0)
            pool.memset(tm[:, :, :], 0.0)
            pool.memset(h2[:, :, :, :, :], 0.0).then_inc(consts, 1)

            pool.wait_ge(kr_sb, 2)

            def key_pair(u, k):
                pool.wait_ge(s_ps, u - 1)
                for i in range(2):
                    key_blocks(pool, 2 * u + i, 2 * (k % 2) + i).then_inc(kbd_ok, 1)

            with pool.Fori(0, PAIRS // BODY - 1) as it:
                for k in range(BODY):
                    key_pair(BODY * it + k + 2, k)
            for u in range(PAIRS - 2, PAIRS):
                key_pair(u, u)

            def split(ins):
                ins.then_inc(gsplit, 1)
                split.n += 1
                pool.wait_ge(gsplit, split.n)

            split.n = 0
            pool.wait_ge(w_late, LATE_ALL)
            for w in range(3):
                pool.tensor_copy(aw[:, w, :].rearrange("p (d h) -> p d h", d=D),
                                 aw_raw[:, w, :].rearrange("p (h d) -> p d h", d=D)).then_inc(aw_ok, 1)
            split(pool.tensor_scalar(grow[:, P:2 * P], grow[:, P:2 * P], 0.5, None, ALU.mult))
            split(pool.tensor_copy(gpart[:, 0, :], grow[:, :]))
            split(pool.tensor_tensor(gres[:, 0, :], grow[:, :], gpart[:, 0, :], ALU.subtract))
            split(pool.tensor_copy(gpart[:, 1, :], gres[:, 0, :]))
            split(pool.tensor_tensor(gres[:, 1, :], gres[:, 0, :], gpart[:, 1, :], ALU.subtract))
            pool.tensor_copy(gpart[:, 2, :], gres[:, 1, :]).then_inc(gsplit, 1)

            def outer(t, p, half):
                a, b = half * D // 2, (half + 1) * D // 2
                if half == 0:
                    pool.wait_ge(k_ready, t + 1)
                at_least(pool, kv_sum, 4 * t - 2 + 2 * half)
                pool.tensor_tensor(
                    kv[:, a * D:b * D, :].rearrange("p (d e) h -> p d e h", d=D // 2),
                    kv[:, D * D + a:D * D + b, :].unsqueeze(2).broadcast_to([P, D // 2, D, H]),
                    qkv[:, p, 2, :, :].unsqueeze(1).broadcast_to([P, D // 2, D, H]), ALU.mult).then_inc(kv_done, 1)

            def weigh(t, p, half):
                a, b = half * D // 2, (half + 1) * D // 2
                pool.wait_ge(kv_sum, 4 * t + 2 + 2 * half)
                if half == 0:
                    pool.wait_ge(qn_done, t + 1)
                    at_least(pool, a_red, 2 * t)
                pool.tensor_tensor(
                    qc[:, a:b, :, :], kvs[:, a * D:b * D, :].rearrange("p (d e) h -> p d e h", d=D // 2),
                    qn[:, p, a:b, :].unsqueeze(2).broadcast_to([P, D // 2, D, H]), ALU.mult).then_inc(qc_done, 1)

            def iteration(t, p, has):
                if has(2):
                    weigh(t + 2, p, 0)
                    weigh(t + 2, p, 1)
                if has(3):
                    outer(t + 3, 1 - p, 0)
                    outer(t + 3, 1 - p, 1)

            pipeline(pool, iteration)

        @block.tensor
        def _(pe):
            def mm(dst, w, rhs, start=True):
                return pe.matmul(dst, w, rhs, start=start, stop=True, skip_group_check=True)

            def x_T(g, half, it):
                pe.wait_ge(x_in[half], 16 * it + 16)
                at_least(pe, xT_sb, g)
                for j in range(GROUP):
                    last = pe.transpose(bank[6][:, j * P:(j + 1) * P], xin[:, half, j, :], ident[:, :])
                last.then_inc(xT_ps, 1)

            def q_of(g):
                pe.wait_ge(xT_sb, g + 1)
                at_least(pe, q_sb, g)
                mm(bank[7][:, :], cwq[:, :], XT[:, ds(GROUP * g, GROUP), :].rearrange("p b s -> p (b s)"))\
                    .then_inc(q_ps, 1)

            pe.wait_ge(ident_ok, 1)
            pe.wait_ge(w_kv, 16 * len(KV))
            pe.transpose(bank[0][:, 0:B], cond_raw[:, :], ident[0:B, 0:B])
            pe.transpose(bank[0][:, B:B + 2], brow_kv[:, :], ident[0:2, 0:2]).then_inc(ct_ps, 1)
            pe.wait_ge(ct_sb, 2)
            mm(bank[1][:, 0:B], cwk[:, :], condT[:, :])
            mm(bank[1][:, B:2 * B], cwv[:, :], condT[:, :]).then_inc(kv_ps, 1)
            x_T(0, 0, 0)
            pe.wait_ge(w_q, 16 * len(Q))
            pe.transpose(bank[0][:, 0:1], brow_q[:, :], ident[0:1, 0:1]).then_inc(bq_ps, 1)
            pe.wait_ge(consts, 1)
            pe.wait_ge(kvm, 1)
            mm(keys_early, rep_d[:, :], kmask[:, :, 0:EARLY]).then_inc(kr_ps, 1)
            q_of(0)
            pe.wait_ge(kvm, 2)
            mm(bank[3][:, 0:D * B], rep_h[:, :], vmask[:, :, :].rearrange("p d b -> p (d b)")).then_inc(vr_ps, 1)

            def scores(u, k, g):
                if k % 2 == 0:
                    pe.wait_ge(q_sb, g + 1)
                if isinstance(u, int) and u == 0:
                    pe.wait_ge(kbd0_ok, 2)
                    pe.wait_ge(bq_sb, 1)
                else:
                    pe.wait_ge(kbd_ok, 2 * u)
                at_least(pe, s_sub, u - 1)
                for i in range(2):
                    j = 2 * (k % 2) + i
                    last = mm(bank[k % 2][:, i * H * H:(i + 1) * H * H], qT[:, k // 2, j * P:(j + 1) * P],
                              kbd[:, j, :, :].rearrange("p h g -> p (h g)"))
                last.then_inc(s_ps, 1)

            def probs_T(u, k):
                pe.wait_ge(s_exp, u + 1)
                at_least(pe, pT_sb, u - 1)
                for j in range(4):
                    last = pe.transpose(bank[2 + k % 2][:, j * P:(j + 1) * P], sexp[:, k % 2, j * P:(j + 1) * P],
                                        ident[:, :])
                last.then_inc(pT_ps, 1)

            def context(u, k):
                pe.wait_ge(pT_sb, u + 1)
                at_least(pe, c_sb, u - 1)
                pe.wait_ge(vbd_ok, u + 1)
                for i in range(2):
                    dst = bank[4 + k % 2][:, i * 144:(i + 1) * 144].rearrange("p (d j l) -> p d j l", d=D + 1, j=2)
                    for j in range(2):
                        last = mm(dst[:, :, j, :], pT[:, k % 2, (2 * i + j) * P:(2 * i + j + 1) * P],
                                  vbd[:, ds(2 * u + i, 1), :, :].rearrange("p o d h -> p (o d) h"))
                last.then_inc(c_ps, 1)

            def first(it, start, end):
                for k in range(BODY):
                    u = BODY * it + k
                    ahead = k % 2 == 0 and not (end and k)
                    if not (end and k == BODY - 1):
                        scores(u + 1, (k + 1) % BODY, 2 * it + (k + 1) // 2)
                    if ahead:
                        q_of(2 * it + k // 2 + 1)
                    probs_T(u, k)
                    if not (start and k == 0):
                        context(u - 1, (k - 1) % BODY)
                    if k % 2 and not end:
                        x_T(2 * it + 2 + k // 2, k // 2, it + 1)

            pe.wait_ge(kr_sb, 1)
            scores(0, 0, 0)
            pe.wait_ge(kvm, 3)
            x_T(1, 1, 0)
            mm(keys_late, rep_d[:, :], kmask[:, :, EARLY:]).then_inc(kr_ps, 1)
            first(0, True, False)
            with pe.Fori(1, PAIRS // BODY - 1) as it:
                first(it, False, False)
            first(PAIRS // BODY - 1, False, True)
            pe.wait_ge(w_late, LATE_ALL)
            pe.wait_ge(xT_sb, B // GROUP)
            pe.transpose(bank[6][:, 0:NE], rout_raw[:, :], ident[0:NE, 0:NE])
            pe.transpose(bank[6][:, NE:NE + 3], brow_o[:, :], ident[0:3, 0:3]).then_inc(rt_ps, 1)
            context(PAIRS - 1, BODY - 1)

            pe.wait_ge(consts, 2)
            pe.wait_ge(aw_ok, 3)
            pe.wait_ge(rt_sb, 3)
            pe.wait_ge(c_sb, PAIRS)

            def h_of(p):
                return h2[:, p, :, :, 1].rearrange("p l b -> p (l b)")

            def y(t):
                at_least(pe, qkv_sb, t)
                mm(QKV[:, 0:P], cwo[:, :], CTXf[:, ds(TOK * t, TOK)]).then_inc(y_ps, 1)

            def qkv_of(t):
                pe.wait_ge(y_sb, t + 1)
                mm(QKV[:, P:], yT[:, :], aw[:, :, :].rearrange("p w n -> p (w n)")).then_inc(qkv_ps, 1)

            def att_T(t):
                pe.wait_ge(a_red, 2 * t + 2)
                at_least(pe, x1_done, t)
                at_least(pe, x1t_sb, t)
                pe.transpose(ATT[:, 0:P], att[:, :, :].rearrange("p h e -> p (h e)"), ident[:, :]).then_inc(aT_ps, 1)

            def project_out(t):
                pe.wait_ge(aT_sb, t + 1)
                mm(ATT[:, P:2 * P], awo[:, :], attT[:, :]).then_inc(p_ps, 1)

            def x_rows(t, p):
                pe.wait_ge(x1_done, t + 1)
                pe.transpose(ATT[:, 2 * P:3 * P], x1T[:, p, :, :].rearrange("p l b -> p (l b)"), ident[:, :])\
                    .then_inc(x1t_ps, 1)

            def gates_x(t, p):
                xs = x1T[:, p, :, :].rearrange("p l b -> p (l b)")
                if isinstance(t, int) and t == 0:
                    pe.wait_ge(gb_in, 16 * 9)
                    pe.wait_ge(h_init, 2)
                pe.wait_ge(x1_done, t + 1)
                at_least(pe, th_done, STEPS * t)
                mm(ZH[:, 0:TOK], hbias[:, :], ones[:, :])
                mm(ZH[:, 0:TOK], gwx[:, 0:P], xs, start=False)
                at_least(pe, to_done, STEPS * t)
                mm(ZO[:, 0:TOK], gwx[:, P:2 * P], xs)

            def memory_x(t, p):
                xs = x1T[:, p, :, :].rearrange("p l b -> p (l b)")
                odd = MEM[:, 1:2 * TOK:2]
                at_least(pe, m_done, STEPS * t)
                mm(MEM[:, 0:2 * TOK], mbias[:, :], pairs[:, :, :].rearrange("p n i -> p (n i)"))
                mm(odd, wxw[:, :], xs, start=False).then_inc(xz_done, 1)

            def logits(t, p):
                pe.wait_ge(h_done, STEPS * t + STEPS)
                at_least(pe, hsq_sb, 2 * t - 1)
                mm(TR[:, 0:NE], h_of(p), routT[:, :]).then_inc(l_ps, 1)

            def hidden(t, p, half):
                pe.wait_ge(h_done, STEPS * t + STEPS)
                if not is_last(t):
                    at_least(pe, hid_sb, 2 * t + half)
                mm(hidden_bank(t, half)[:, :], h_of(p), w1[:, 4 * half:4 * half + 4, :].rearrange("p e d -> p (e d)"))\
                    .then_inc(hid_ps, 1)

            def hidden_T(t, half):
                pe.wait_ge(hid_sb, 2 * t + half + 1)
                at_least(pe, hsq_sb, 2 * t + half)
                if half and not is_last(t):
                    pe.wait_ge(l_sb, t + 2)
                for j in range(4):
                    last = pe.transpose(TR[:, j * P:(j + 1) * P], hid[:, half, j, :], ident[:, :])
                last.then_inc(hT_ps, 1)

            def experts_out(t, half):
                pe.wait_ge(hsq_sb, 2 * t + half + 1)
                if half == 0 and not is_last(t):
                    at_least(pe, res_done, NE * t)
                for j in range(4):
                    last = mm(out_bank(t)[:, 0:C], hsq[:, half, j * P:(j + 1) * P], w2[:, 4 * half + j, :],
                              start=half == 0 and j == 0)
                last.then_inc(o_ps, 1)

            def step(t, p, s):
                at_least(pe, h_done, STEPS * t + s)
                h = h2[:, p, s - 1, :, 1] if s else h2[:, 1 - p, STEPS - 1, :, 1]
                col = s * B
                mm(ZH[:, col:col + B], gwh[:, 0:P], h, start=False).then_inc(zh_ps, 1)
                mm(MEM[:, 2 * s * B:2 * (s + 1) * B], whw[:, :], h.unsqueeze(2).broadcast_to([P, B, 2]),
                   start=False).then_inc(g_ps, 1)
                mm(ZO[:, col:col + B], gwh[:, P:2 * P], h, start=False).then_inc(zo_ps, 1)

            def after(t, p, has):
                q = 1 - p
                if has(-1):
                    logits(t - 1, q)
                    hidden(t - 1, q, 0)
                    experts_out(t - 2, 0)
                    hidden_T(t - 2, 1)
                    hidden(t - 1, q, 1)
                    hidden_T(t - 1, 0)
                    experts_out(t - 2, 1)
                else:
                    hidden_T(t - 2, 1)
                    experts_out(t - 2, 0)
                    experts_out(t - 2, 1)

            def iteration(t, p, has):
                if has(-2) and not has(0):
                    return after(t, p, has)
                q = 1 - p
                if has(0):
                    step(t, p, 0)
                if has(-1):
                    logits(t - 1, q)
                if has(4):
                    y(t + 4)
                if has(-2):
                    experts_out(t - 2, 0)
                if has(1):
                    att_T(t + 1)
                if has(0):
                    step(t, p, 1)
                if has(1):
                    project_out(t + 1)
                if has(-2):
                    hidden_T(t - 2, 1)
                if has(-1):
                    hidden(t - 1, q, 0)
                if has(0):
                    step(t, p, 2)
                if has(4):
                    qkv_of(t + 4)
                if has(-2):
                    experts_out(t - 2, 1)
                if has(0):
                    step(t, p, 3)
                if has(1):
                    x_rows(t + 1, q)
                if has(-1):
                    hidden_T(t - 1, 0)
                    hidden(t - 1, q, 1)
                if has(1):
                    gates_x(t + 1, q)
                    memory_x(t + 1, q)

            pipeline(pe, iteration)

        @block.scalar
        def _(act):
            act.preload_act_table(ACT.Exp)

            def group_T(g):
                act.wait_ge(xT_ps, g + 1)
                act.activation(XT[:, ds(GROUP * g, GROUP), :].rearrange("p b s -> p (b s)"), bank[6][:, :], ACT.Copy)\
                    .then_inc(xT_sb, 1)

            def group_q(g, half):
                act.wait_ge(q_ps, g + 1)
                at_least(act, s_ps, 2 * (g - 1))
                act.activation(qT[:, half, :], bank[7][:, :], ACT.Identity, bias=bcol[:, 0:1]).then_inc(q_sb, 1)

            def exps(u, k):
                act.wait_ge(s_sub, u + 1)
                at_least(act, pT_ps, u - 1)
                act.activation(sexp[:, k % 2, :], ssub[:, k % 2, :, :].rearrange("p h g -> p (h g)"), ACT.Exp,
                               scale=SCALE).then_inc(s_exp, 1)

            def probs_out(u, k):
                act.wait_ge(pT_ps, u + 1)
                at_least(act, c_ps, u - 1)
                act.activation(pT[:, k % 2, :], bank[2 + k % 2][:, :], ACT.Copy).then_inc(pT_sb, 1)

            def first(it, end):
                for k in range(BODY):
                    ahead = k % 2 == 0 and not (end and k)
                    exps(BODY * it + k, k)
                    if ahead:
                        group_q(2 * it + k // 2 + 1, 1 - k // 2)
                    probs_out(BODY * it + k, k)
                    if k % 2 and not end:
                        group_T(2 * it + 2 + k // 2)

            act.wait_ge(ct_ps, 1)
            act.activation(condT[:, :], bank[0][:, 0:B], ACT.Copy).then_inc(ct_sb, 1)
            act.activation(bcol[:, 1:3], bank[0][:, B:B + 2], ACT.Copy).then_inc(ct_sb, 1)
            act.wait_ge(kv_ps, 1)
            act.wait_ge(ct_sb, 2)
            for i in range(2):
                act.activation(kvT[:, i, :], bank[1][:, i * B:(i + 1) * B], ACT.Identity, bias=bcol[:, i + 1:i + 2])\
                    .then_inc(kv_sb, 1)
            group_T(0)
            act.wait_ge(bq_ps, 1)
            act.activation(bcol[:, 0:1], bank[0][:, 0:1], ACT.Copy).then_inc(bq_sb, 1)
            act.wait_ge(kr_ps, 1)
            act.activation(kr[:, :, 0:EARLY], keys_early, ACT.Copy).then_inc(kr_sb, 1)
            act.wait_ge(bq_sb, 1)
            group_q(0, 0)
            act.wait_ge(vr_ps, 1)
            act.activation(vr[:, 0:D, :].rearrange("p d b -> p (d b)"), bank[3][:, 0:D * B], ACT.Copy)\
                .then_inc(vr_sb, 1)
            group_T(1)
            act.wait_ge(kr_ps, 2)
            act.activation(kr[:, :, EARLY:], keys_late, ACT.Copy).then_inc(kr_sb, 1)
            first(0, False)
            with act.Fori(1, PAIRS // BODY - 1) as it:
                first(it, False)
            first(PAIRS // BODY - 1, True)
            act.wait_ge(rt_ps, 1)
            act.activation(routT[:, :], bank[6][:, 0:NE], ACT.Copy).then_inc(rt_sb, 1)
            act.activation(bcol[:, 3:5], bank[6][:, NE:NE + 2], ACT.Copy).then_inc(rt_sb, 1)
            act.activation(gcol[:, :], bank[6][:, NE + 2:NE + 3], ACT.Copy, scale=0.5).then_inc(rt_sb, 1)

            def y_out(t):
                act.wait_ge(y_ps, t + 1)
                at_least(act, qkv_ps, t)
                act.activation(yT[:, :], QKV[:, 0:P], ACT.Identity, bias=bcol[:, 3:4]).then_inc(y_sb, 1)

            def qkv_out(t, p):
                act.wait_ge(qkv_ps, t + 1)
                at_least(act, kv_done, 2 * (t - 1))
                act.activation(nk[:, p, :, :].rearrange("p d h -> p (d h)"), QKV[:, 2 * P:3 * P], ACT.Relu, scale=-1.0)\
                    .then_inc(nk_done, 1)
                act.activation(qkv[:, p, :, :, :].rearrange("p w d h -> p (w d h)"), QKV[:, P:], ACT.Copy)\
                    .then_inc(qkv_sb, 1)

            def exp_qk(t, p):
                act.wait_ge(ex_ready, t + 1)
                act.wait_ge(nk_done, t + 1)
                at_least(act, qn_done, t - 1)
                act.activation(ex[:, p, 0, :, :], ex_in[:, :, :], ACT.Exp)
                act.activation(ex[:, p, 1, :, :], nk[:, p, :, :], ACT.Exp, scale=-1.0).then_inc(ex_done, 1)

            def att_out(t):
                act.wait_ge(aT_ps, t + 1)
                at_least(act, p_ps, t)
                act.activation(attT[:, :], ATT[:, 0:P], ACT.Copy).then_inc(aT_sb, 1)

            def x_rows_out(t):
                act.wait_ge(x1t_ps, t + 1)
                act.activation(x1[:, ds(t, 1), :].rearrange("p o c -> p (o c)"), ATT[:, 2 * P:3 * P], ACT.Copy)\
                    .then_inc(x1t_sb, 1)

            def relu(t, p, half, some):
                if some == 0:
                    act.wait_ge(hid_ps, 2 * t + half + 1)
                    act.wait_ge(gw_done, t + 1)
                    at_least(act, hT_ps, 2 * t + half - 1)
                for j in range(2 * some, 2 * some + 2):
                    e = 4 * half + j
                    last = act.activation(hid[:, half, j, :], hidden_bank(t, half)[:, j * DE:(j + 1) * DE], ACT.Relu,
                                          scale=gw[:, p, e:e + 1])
                if some:
                    last.then_inc(hid_sb, 1)

            def square(t, half):
                act.wait_ge(hT_ps, 2 * t + half + 1)
                at_least(act, o_ps, 2 * t + half - 1)
                act.activation(hsq[:, half, :], TR[:, :], ACT.Square).then_inc(hsq_sb, 1)

            def taken_sum(t, p):
                act.wait_ge(gw_done, t + 1)
                at_least(act, gr_done, t)
                act.activation(gw2[:, :], gw[:, p, :], ACT.Square, accum_out=gsum[:, :]).then_inc(gs_done, 1)

            def gate_exp(t):
                act.wait_ge(l_dl, t + 1)
                at_least(act, gw_done, t)
                act.activation(gex[:, :, :], dl[:, :, :], ACT.Exp, scale=0.5).then_inc(g_exp, 1)

            def gates(t, p, s):
                n = STEPS * t + s
                col = s * B
                act.wait_ge(zh_ps, n + 1)
                act.activation(th[:, :, 1], ZH[:, col:col + B], ACT.Tanh, scale=0.5).then_inc(th_done, 1)
                act.wait_ge(zo_ps, n + 1)
                act.activation(to[:, :], ZO[:, col:col + B], ACT.Tanh, bias=gcol[:, 0:1], scale=0.5)\
                    .then_inc(to_done, 1)

            def memory_tanh(t, s):
                n = STEPS * t + s
                act.wait_ge(m_done, n + 1)
                act.activation(tm[:, :, 1], mem[:, :, 1], ACT.Tanh).then_inc(tm_done, 1)

            def after(t, p, has):
                q = 1 - p
                if has(-1):
                    relu(t - 2, p, 1, 1)
                    gate_exp(t - 1)
                    relu(t - 1, q, 0, 0)
                    relu(t - 1, q, 0, 1)
                    square(t - 2, 1)
                    relu(t - 1, q, 1, 0)
                    relu(t - 1, q, 1, 1)
                    square(t - 1, 0)
                    taken_sum(t - 1, q)
                else:
                    square(t - 2, 1)

            def iteration(t, p, has):
                if has(-2) and not has(0):
                    return after(t, p, has)
                q = 1 - p
                if has(0):
                    gates(t, p, 0)
                    memory_tanh(t, 0)
                if has(4):
                    y_out(t + 4)
                if has(-2):
                    relu(t - 2, p, 1, 1)
                if has(1):
                    att_out(t + 1)
                if has(0):
                    gates(t, p, 1)
                if has(-1):
                    gate_exp(t - 1)
                if has(0):
                    memory_tanh(t, 1)
                if has(3):
                    exp_qk(t + 3, q)
                if has(-2):
                    square(t - 2, 1)
                if has(0):
                    gates(t, p, 2)
                    memory_tanh(t, 2)
                if has(-1):
                    relu(t - 1, q, 0, 0)
                    relu(t - 1, q, 0, 1)
                    taken_sum(t - 1, q)
                if has(0):
                    gates(t, p, 3)
                if has(1):
                    x_rows_out(t + 1)
                if has(4):
                    qkv_out(t + 4, p)
                if has(0):
                    memory_tanh(t, 3)
                if has(-1):
                    square(t - 1, 0)
                    relu(t - 1, q, 1, 0)

            pipeline(act, iteration)

        @block.vector
        def _(dve):
            dve.wait_ge(ident_ok, 1)
            dve.tensor_reduce(m_dim[:, :], ident[:, :].rearrange("p (h d) -> p d h", d=D), AX.X, ALU.add)\
                .then_inc(m_dim_ok, 1)
            dve.wait_ge(consts, 1)
            dve.wait_ge(kv_sb, 1)
            def key_mask(a, b):
                dve.tensor_tensor(kmask[:, :, a:b], m_head[:, :].unsqueeze(2).broadcast_to([P, H, b - a]),
                                  kvT[:, 0, a:b].unsqueeze(1).broadcast_to([P, H, b - a]), ALU.mult).then_inc(kvm, 1)

            key_mask(0, EARLY)
            dve.wait_ge(kv_sb, 2)
            dve.tensor_tensor(vmask[:, :, :], m_dim[:, :].unsqueeze(2).broadcast_to([P, D, B]),
                              kvT[:, 1, :].unsqueeze(1).broadcast_to([P, D, B]), ALU.mult).then_inc(kvm, 1)
            key_mask(EARLY, B)

            def largest(u, k):
                dve.wait_ge(s_ps, u + 1)
                dve.tensor_reduce(smax[:, k % 2, :], bank[k % 2][:, :].rearrange("p (h g) -> p h g", g=H), AX.X,
                                  ALU.max).then_inc(s_max, 1)

            def less_largest(u, k):
                dve.wait_ge(s_max, u + 1)
                at_least(dve, s_exp, u - 1)
                dve.tensor_tensor(ssub[:, k % 2, :, :], bank[k % 2][:, :].rearrange("p (h g) -> p h g", g=H),
                                  smax[:, k % 2, :].unsqueeze(2).broadcast_to([P, 2 * H, H]), ALU.subtract)\
                    .then_inc(s_sub, 1)

            def context_of(k):
                return bank[4 + k % 2][:, 0:288].rearrange("p (i d h) -> p i d h", i=2, d=D + 1)

            def inverse_sum(u, k):
                dve.wait_ge(c_ps, u + 1)
                dve.reciprocal(srec[:, k % 2, :, :], context_of(k)[:, :, D, :]).then_inc(c_rec, 1)

            def normalise(u, k):
                dve.wait_ge(c_rec, u + 1)
                dve.tensor_tensor(CTX[:, :, ds(2 * u, 2)].rearrange("p (d h) i -> p i d h", d=D),
                                  context_of(k)[:, :, 0:D, :],
                                  srec[:, k % 2, :, :].unsqueeze(2).broadcast_to([P, 2, D, H]), ALU.mult)\
                    .then_inc(c_sb, 1)

            def value_blocks(u):
                dve.tensor_tensor(vbd[:, ds(2 * u, 2), :, :], vr[:, :, ds(2 * u, 2)].rearrange("p d b -> p b d")
                                  .unsqueeze(3).broadcast_to([P, 2, D + 1, D]),
                                  m_hl[:, :].unsqueeze(1).unsqueeze(1).broadcast_to([P, 2, D + 1, D]), ALU.mult)\
                    .then_inc(vbd_ok, 1)

            def first(it, start, end):
                for k in range(BODY):
                    u = BODY * it + k
                    more = not (end and k == BODY - 1)
                    if more:
                        largest(u + 1, k + 1)
                    if not (start and k < 2):
                        normalise(u - 2, k)
                    if more:
                        less_largest(u + 1, k + 1)
                        value_blocks(u + 1)
                    if not (start and k == 0):
                        inverse_sum(u - 1, k - 1)

            dve.wait_ge(kr_sb, 1)
            for b in range(2):
                key_blocks(dve, b, b).then_inc(kbd0_ok, 1)
            dve.wait_ge(vr_sb, 1)
            value_blocks(0)
            largest(0, 0)
            less_largest(0, 0)
            first(0, True, False)
            with dve.Fori(1, PAIRS // BODY - 1) as it:
                first(it, False, False)
            first(PAIRS // BODY - 1, False, True)
            inverse_sum(PAIRS - 1, BODY - 1)
            normalise(PAIRS - 2, BODY - 2)
            normalise(PAIRS - 1, BODY - 1)
            dve.wait_ge(consts, 2)
            dve.wait_ge(w_late, LATE_ALL)
            dve.tensor_scalar(whw[:, :], whw_raw[:, :], 0.5, None, ALU.mult).then_inc(h_init, 1)
            dve.tensor_copy(h2[:, 1, STEPS - 1, :, 1], condT[:, :]).then_inc(h_init, 1)

            def flat(ap):
                return ap.rearrange("p a b -> p (a b)")

            def head_max(t, p):
                dve.wait_ge(qkv_sb, t + 1)
                dve.tensor_reduce(qmax[:, :], qkv[:, p, 0, :, :].rearrange("p d h -> p h d"), AX.X, ALU.max)\
                    .then_inc(q_max, 1)

            def less_max(t, p):
                at_least(dve, ex_done, t)
                dve.wait_ge(q_max, t + 1)
                dve.tensor_tensor(ex_in[:, :, :], qkv[:, p, 0, :, :],
                                  qmax[:, :].unsqueeze(1).broadcast_to([P, D, H]), ALU.subtract).then_inc(ex_ready, 1)

            def keys(t, p):
                dve.wait_ge(ex_done, t + 1)
                at_least(dve, kv_done, 2 * t)
                dve.scalar_tensor_tensor(out=kv[:, D * D:, :], in0=qkv[:, p, 1, :, :], scalar=0.0,
                                         in1=ex[:, p, 1, :, :], op0=ALU.max, op1=ALU.add).then_inc(k_ready, 1)

            def query_sum(t, p):
                dve.tensor_reduce(qsum[:, :], ex[:, p, 0, :, :].rearrange("p d h -> p h d"), AX.X, ALU.add)\
                    .then_inc(q_sum, 1)

            def key_sums(t):
                dve.wait_ge(k_ready, t + 1)
                dve.tensor_tensor_scan(flat(kvs[:, D * D:, :]), flat(scan_mask[:, D * D:, :]), flat(kv[:, D * D:, :]),
                                       0.0, ALU.mult, ALU.add).then_inc(k_sum, 1)

            def divisors(t):
                dve.wait_ge(q_sum, t + 1)
                dve.wait_ge(k_sum, t + 1)
                dve.scalar_tensor_tensor(out=den[:, :, :], in0=kvs[:, D * D:, :], scalar=EPS,
                                         in1=qsum[:, :].unsqueeze(1).broadcast_to([P, D, H]), op0=ALU.add,
                                         op1=ALU.mult).then_inc(d_den, 1)

            def inverses(t, half):
                a, b = half * D // 2, (half + 1) * D // 2
                dve.wait_ge(d_den, t + 1)
                dve.reciprocal(rden[:, a:b, :], den[:, a:b, :]).then_inc(d_rec, 1)

            def queries(t, p):
                dve.wait_ge(d_rec, 2 * t + 2)
                at_least(dve, qc_done, 2 * (t - 1))
                dve.tensor_tensor(qn[:, p, :, :], ex[:, p, 0, :, :], rden[:, :, :], ALU.mult).then_inc(qn_done, 1)

            def sum_heads(t, part):
                a, b = part * D * D // 4, (part + 1) * D * D // 4
                if part % 2 == 0:
                    dve.wait_ge(kv_done, 2 * t + part // 2 + 1)
                    at_least(dve, qc_done, 2 * t - 1 + part // 2)
                dve.tensor_tensor_scan(flat(kvs[:, a:b, :]), flat(scan_mask[:, a:b, :]), flat(kv[:, a:b, :]), 0.0,
                                       ALU.mult, ALU.add).then_inc(kv_sum, 1)

            def add_dims(t, half):
                a, b = half * D // 2, (half + 1) * D // 2
                if half == 0:
                    dve.wait_ge(qc_done, 2 * t + 2)
                    at_least(dve, aT_ps, t)
                dve.tensor_reduce(att[:, :, a:b].rearrange("p h e -> p e h"),
                                  qc[:, :, a:b, :].rearrange("p d e h -> p e h d"), AX.X, ALU.add).then_inc(a_red, 1)

            def residual(t, p):
                dve.wait_ge(p_ps, t + 1)
                at_least(dve, x1t_ps, t - 1)
                at_least(dve, xz_done, t - 1)
                dve.scalar_tensor_tensor(out=x1T[:, p, :, :],
                                         in0=ATT[:, P:2 * P].rearrange("p (l b) -> p l b", b=B),
                                         scalar=bcol[:, 4:5], in1=XTt[:, ds(STEPS * t, STEPS), :],
                                         op0=ALU.add, op1=ALU.add).then_inc(x1_done, 1)

            def route(t):
                dve.wait_ge(l_ps, t + 1)
                dve.tensor_copy(lg[:, 0, :], TR[:, 0:NE]).then_inc(l_copy, 1)
                dve.max(top[:, :], TR[:, 0:NE]).then_inc(l_sb, 1)

            def two_largest(t):
                dve.wait_ge(l_sb, t + 1)
                dve.tensor_copy(lead[:, 0:2], top[:, 0:2]).then_inc(l_lead, 1)

            def take_out(t):
                dve.match_replace(lg[:, 1, :], lead[:, :], lg[:, 0, :], NONE).then_inc(l_out, 1)

            def less_top(t):
                dve.wait_ge(l_out, t + 1)
                at_least(dve, g_exp, t)
                dve.tensor_scalar(dl[:, :, :], lg[:, :, :], top[:, 0:1], None, ALU.subtract).then_inc(l_dl, 1)

            def taken(t, p):
                dve.wait_ge(g_exp, t + 1)
                at_least(dve, hid_sb, 2 * (t - 1))
                dve.tensor_tensor(gw[:, p, :], gex[:, 0, :], gex[:, 1, :], ALU.subtract).then_inc(gw_done, 1)

            def taken_inverse(t, p):
                dve.wait_ge(gs_done, t + 1)
                dve.reciprocal(grec[:, p:p + 1], gsum[:, :]).then_inc(gr_done, 1)

            def finish(t, p):
                dve.wait_ge(o_ps, 2 * t + 2)
                dve.wait_ge(gr_done, t + 1)
                dve.wait_ge(x1t_sb, t + 1)
                at_least(dve, out_done, 16 * (t - 1))
                dve.scalar_tensor_tensor(out=res[:, p, :], in0=out_bank(t)[:, 0:C], scalar=grec[:, p:p + 1],
                                         in1=x1[:, ds(t, 1), :].rearrange("p o c -> p (o c)"), op0=ALU.mult,
                                         op1=ALU.add).then_inc(res_done, NE)

            def memory(t, p, s):
                n = STEPS * t + s
                dve.wait_ge(th_done, n + 1)
                dve.wait_ge(g_ps, n + 1)
                dve.tensor_tensor_scan(flat(mem[:, :, :]), flat(th[:, :, :]), MEM[:, 2 * s * B:2 * (s + 1) * B],
                                       0.0, ALU.mult, ALU.add).then_inc(m_done, 1)

            def renewed(t, s):
                n = STEPS * t + s
                dve.wait_ge(to_done, n + 1)
                dve.tensor_scalar(wo[:, :, 0], to[:, :], -0.5, 0.5, ALU.mult, ALU.add).then_inc(w_done, 1)

            def kept(t, p, s):
                n = STEPS * t + s
                h = h2[:, p, s - 1, :, 1] if s else h2[:, 1 - p, STEPS - 1, :, 1]
                dve.wait_ge(w_done, n + 1)
                dve.scalar_tensor_tensor(out=wo[:, :, 1], in0=wo[:, :, 0], scalar=1.0, in1=h, op0=ALU.subtract,
                                         op1=ALU.mult, reverse0=True).then_inc(oh_done, 1)

            def new_h(t, p, s):
                n = STEPS * t + s
                dve.wait_ge(tm_done, n + 1)
                dve.wait_ge(oh_done, n + 1)
                dve.tensor_tensor_scan(flat(h2[:, p, s, :, :]), flat(tm[:, :, :]), flat(wo[:, :, :]), 0.0, ALU.mult,
                                       ALU.add).then_inc(h_done, 1)

            def iteration(t, p, has):
                q = 1 - p
                if has(0):
                    memory(t, p, 0)
                    renewed(t, 0)
                if has(-1):
                    route(t - 1)
                if has(0):
                    kept(t, p, 0)
                if has(3):
                    head_max(t + 3, q)
                if has(0):
                    new_h(t, p, 0)
                if has(-1):
                    two_largest(t - 1)
                if has(2):
                    sum_heads(t + 2, 0)
                if has(-1):
                    dve.wait_ge(l_lead, t)
                    dve.wait_ge(l_copy, t)
                if has(2):
                    sum_heads(t + 2, 1)
                elif has(-1):
                    dve.tensor_copy(gw2[:, 0:1], lead[:, 0:1])
                if has(-1):
                    take_out(t - 1)
                    less_top(t - 1)
                if has(0):
                    memory(t, p, 1)
                    renewed(t, 1)
                if has(3):
                    less_max(t + 3, q)
                if has(0):
                    kept(t, p, 1)
                if has(2):
                    queries(t + 2, p)
                if has(0):
                    new_h(t, p, 1)
                if has(2):
                    sum_heads(t + 2, 2)
                if has(-1):
                    taken(t - 1, q)
                if has(2):
                    sum_heads(t + 2, 3)
                if has(0):
                    memory(t, p, 2)
                if has(3):
                    keys(t + 3, q)
                if has(0):
                    renewed(t, 2)
                    kept(t, p, 2)
                if has(3):
                    query_sum(t + 3, q)
                if has(0):
                    new_h(t, p, 2)
                if has(3):
                    key_sums(t + 3)
                if has(1):
                    residual(t + 1, q)
                if has(3):
                    divisors(t + 3)
                    inverses(t + 3, 0)
                if has(0):
                    memory(t, p, 3)
                if has(-2):
                    finish(t - 2, p)
                if has(0):
                    renewed(t, 3)
                if has(-1):
                    taken_inverse(t - 1, q)
                if has(0):
                    kept(t, p, 3)
                    new_h(t, p, 3)
                if has(3):
                    inverses(t + 3, 1)
                if has(2):
                    add_dims(t + 2, 0)
                    add_dims(t + 2, 1)

            pipeline(dve, iteration)


_INS = ["x", "cond_1024", "L0_cond_Wq", "L0_cond_bq", "L0_cond_Wk", "L0_cond_bk", "L0_cond_Wv", "L0_cond_bv",
        "L0_cond_Wo", "L0_cond_bo", "L0_attn_Wq", "L0_attn_Wk", "L0_attn_Wv", "L0_attn_Wo", "L0_attn_bo",
        "L0_cond2_w_W", "L0_cond2_w_b", "L0_cond2_wx_W", "L0_cond2_wx_b", "L0_cond2_wh_W", "L0_cond2_wh_b",
        "L0_ffn_router_w", "L0_ffn_w1_all", "L0_ffn_w2_all"]
_OUTS = [((B, S, C), "float32")]


def kernel(**inputs):
    import numpy as _np
    import concourse.bacc as _bacc
    from concourse import mybir as _mybir
    from concourse.bass_utils import run_bass_kernel_spmd as _run

    nc = _bacc.Bacc("TRN2", target_bir_lowering=False, num_devices=1)
    arrays, args = {}, []
    for name in _INS:
        a = _np.ascontiguousarray(inputs[name])
        arrays[f"in_{name}_dram"] = a
        args.append(nc.dram_tensor(f"in_{name}_dram", a.shape, _mybir.dt.from_np(a.dtype), kind="ExternalInput").ap())
    for i, (shape, dtype) in enumerate(_OUTS):
        dt = _mybir.dt.from_np(_np.dtype(dtype))
        args.append(nc.dram_tensor(f"out_{i}_dram", shape, dt, kind="ExternalOutput").ap())
    adaln_attention_recurrence_moe(nc, *args)
    r = _run(nc, [arrays], core_ids=[0])
    return r.results[0]["out_0_dram"]
```
